# Optimizing a Trainium2 kernel written in Bass

```python
import numpy as np
import jax
import jax.numpy as jnp

def _softmax(x, axis=-1):
    return jax.nn.softmax(x, axis=axis)

def _gelu(x):
    return jax.nn.gelu(x, approximate=True)

def _silu(x):
    return jax.nn.silu(x)

def _sigmoid(x):
    return jax.nn.sigmoid(x)

def _layernorm(x, axis=-1, eps=1e-05):
    m = jnp.mean(x, axis=axis, keepdims=True)
    v = jnp.var(x, axis=axis, keepdims=True)
    return (x - m) / jnp.sqrt(v + eps)

def _scatter_add(tgt, idx, src, axis=0):
    return tgt.at[idx].add(src)

def _segment_sum(src, seg, n):
    return jax.ops.segment_sum(src, seg, n)
kernel_name = 'mk_seq_postln_d1_jaxref_r8_a94ffe'

def setup_inputs(seed: int=0):
    np.random.seed(seed)
    _w = jnp.asarray

    def _L0_attn_setup():
        import jax, jax.numpy as jnp
        import numpy as np
        from jax import lax
        D_MODEL = 128
        D_STATE = 16
        D_CONV = 4
        EXPAND = 2
        D_INNER = EXPAND * D_MODEL
        DT_RANK = (D_MODEL + 15) // 16
        BATCH = 2
        SEQLEN = 128

        def _layernorm(x, g, b, eps=1e-05):
            mu = jnp.mean(x, axis=-1, keepdims=True)
            var = jnp.mean(jnp.square(x - mu), axis=-1, keepdims=True)
            return (x - mu) * lax.rsqrt(var + eps) * g + b

        def _mamba(x, in_proj_w, conv_w, conv_b, x_proj_w, dt_proj_w, dt_proj_b, A_log, D, out_proj_w):
            Bsz, L, _ = x.shape
            xz = x @ in_proj_w.T
            xi, z = jnp.split(xz, 2, axis=-1)
            xc = xi.transpose(0, 2, 1)
            xc = lax.conv_general_dilated(xc, conv_w, window_strides=(1,), padding=[(D_CONV - 1, 0)], feature_group_count=D_INNER, dimension_numbers=('NCH', 'OIH', 'NCH'))
            xc = xc + conv_b[None, :, None]
            xc = jax.nn.silu(xc).transpose(0, 2, 1)
            x_dbl = xc @ x_proj_w.T
            dt, Bmat, Cmat = jnp.split(x_dbl, [DT_RANK, DT_RANK + D_STATE], axis=-1)
            dt = jax.nn.softplus(dt @ dt_proj_w.T + dt_proj_b)
            A = -jnp.exp(A_log)
            dA = jnp.exp(dt[..., None] * A)
            dBx = dt[..., None] * Bmat[:, :, None, :] * xc[..., None]

            def step(h, inp):
                dA_t, dBx_t, C_t = inp
                h = dA_t * h + dBx_t
                y = jnp.einsum('bdn,bn->bd', h, C_t)
                return (h, y)
            h0 = jnp.zeros((Bsz, D_INNER, D_STATE), x.dtype)
            _, ys = lax.scan(step, h0, (dA.transpose(1, 0, 2, 3), dBx.transpose(1, 0, 2, 3), Cmat.transpose(1, 0, 2)))
            y = ys.transpose(1, 0, 2)
            y = y + D * xc
            y = y * jax.nn.silu(z)
            return y @ out_proj_w.T
        key = jax.random.key(seed)
        ks = jax.random.split(key, 12)
        s = lambda k, shape, sc=0.02: jax.random.normal(k, shape, jnp.float32) * sc
        A_log = jnp.log(jnp.tile(jnp.arange(1, D_STATE + 1, dtype=jnp.float32), (D_INNER, 1)))
        dt_bias = jnp.log(jnp.expm1(jnp.full((D_INNER,), 0.01, jnp.float32)))
        return {'x': jax.random.normal(ks[0], (BATCH, SEQLEN, D_MODEL), jnp.float32), 'in_proj_w': s(ks[1], (2 * D_INNER, D_MODEL)), 'conv_w': s(ks[2], (D_INNER, 1, D_CONV), 0.1), 'conv_b': s(ks[3], (D_INNER,), 0.1), 'x_proj_w': s(ks[4], (DT_RANK + 2 * D_STATE, D_INNER)), 'dt_proj_w': s(ks[5], (D_INNER, DT_RANK), 0.1), 'dt_proj_b': dt_bias, 'A_log': A_log, 'D': jnp.ones((D_INNER,), jnp.float32), 'out_proj_w': s(ks[6], (D_MODEL, D_INNER)), 'ln1_g': jnp.ones((D_MODEL,), jnp.float32), 'ln1_b': jnp.zeros((D_MODEL,), jnp.float32), 'ln2_g': jnp.ones((D_MODEL,), jnp.float32), 'ln2_b': jnp.zeros((D_MODEL,), jnp.float32), 'ffn_w1': s(ks[7], (4 * D_MODEL, D_MODEL)), 'ffn_b1': jnp.zeros((4 * D_MODEL,), jnp.float32), 'ffn_w2': s(ks[8], (D_MODEL, 4 * D_MODEL)), 'ffn_b2': jnp.zeros((D_MODEL,), jnp.float32)}
    _L0_attn_in = _L0_attn_setup()

    def _L0_ffn_setup():
        import jax, jax.numpy as jnp
        import numpy as np
        NUM_EXPERTS = 8
        HIDDEN = 128
        FFN = 512
        BATCH = 2
        SEQ = 256
        key = jax.random.key(seed)
        k_x, k_g, k_u, k_d = jax.random.split(key, 4)
        scale_in = 1.0 / np.sqrt(HIDDEN)
        scale_mid = 1.0 / np.sqrt(FFN)
        return {'hidden_states': jax.random.normal(k_x, (BATCH, SEQ, HIDDEN), dtype=jnp.float32), 'Wg': jax.random.normal(k_g, (NUM_EXPERTS, HIDDEN, FFN), dtype=jnp.float32) * scale_in, 'Wu': jax.random.normal(k_u, (NUM_EXPERTS, HIDDEN, FFN), dtype=jnp.float32) * scale_in, 'Wd': jax.random.normal(k_d, (NUM_EXPERTS, FFN, HIDDEN), dtype=jnp.float32) * scale_mid}
    _L0_ffn_in = _L0_ffn_setup()
    _d = {'L0_attn_x': _L0_attn_in['x'], 'L0_attn_in_proj_w': _L0_attn_in['in_proj_w'], 'L0_attn_conv_w': _L0_attn_in['conv_w'], 'L0_attn_conv_b': _L0_attn_in['conv_b'], 'L0_attn_x_proj_w': _L0_attn_in['x_proj_w'], 'L0_attn_dt_proj_w': _L0_attn_in['dt_proj_w'], 'L0_attn_dt_proj_b': _L0_attn_in['dt_proj_b'], 'L0_attn_A_log': _L0_attn_in['A_log'], 'L0_attn_D': _L0_attn_in['D'], 'L0_attn_out_proj_w': _L0_attn_in['out_proj_w'], 'L0_attn_ln1_g': _L0_attn_in['ln1_g'], 'L0_attn_ln1_b': _L0_attn_in['ln1_b'], 'L0_attn_ln2_g': _L0_attn_in['ln2_g'], 'L0_attn_ln2_b': _L0_attn_in['ln2_b'], 'L0_attn_ffn_w1': _L0_attn_in['ffn_w1'], 'L0_attn_ffn_b1': _L0_attn_in['ffn_b1'], 'L0_attn_ffn_w2': _L0_attn_in['ffn_w2'], 'L0_attn_ffn_b2': _L0_attn_in['ffn_b2'], 'L0_ffn_Wg': _L0_ffn_in['Wg'], 'L0_ffn_Wu': _L0_ffn_in['Wu'], 'L0_ffn_Wd': _L0_ffn_in['Wd']}
    _x0 = _d['L0_attn_x']
    _d['L0_attn_x'] = jax.random.normal(jax.random.fold_in(jax.random.key(seed), 1), (16, 256, 128), dtype=_x0.dtype)
    del _x0
    return _d

def reference(L0_attn_x, L0_attn_in_proj_w, L0_attn_conv_w, L0_attn_conv_b, L0_attn_x_proj_w, L0_attn_dt_proj_w, L0_attn_dt_proj_b, L0_attn_A_log, L0_attn_D, L0_attn_out_proj_w, L0_attn_ln1_g, L0_attn_ln1_b, L0_attn_ln2_g, L0_attn_ln2_b, L0_attn_ffn_w1, L0_attn_ffn_b1, L0_attn_ffn_w2, L0_attn_ffn_b2, L0_ffn_Wg, L0_ffn_Wu, L0_ffn_Wd):

    def _L0_attn_ref(x, in_proj_w, conv_w, conv_b, x_proj_w, dt_proj_w, dt_proj_b, A_log, D, out_proj_w, ln1_g, ln1_b, ln2_g, ln2_b, ffn_w1, ffn_b1, ffn_w2, ffn_b2):
        import jax, jax.numpy as jnp
        import numpy as np
        from jax import lax
        D_MODEL = 128
        D_STATE = 16
        D_CONV = 4
        EXPAND = 2
        D_INNER = EXPAND * D_MODEL
        DT_RANK = (D_MODEL + 15) // 16
        BATCH = 2
        SEQLEN = 128

        def _layernorm(x, g, b, eps=1e-05):
            mu = jnp.mean(x, axis=-1, keepdims=True)
            var = jnp.mean(jnp.square(x - mu), axis=-1, keepdims=True)
            return (x - mu) * lax.rsqrt(var + eps) * g + b

        def _mamba(x, in_proj_w, conv_w, conv_b, x_proj_w, dt_proj_w, dt_proj_b, A_log, D, out_proj_w):
            Bsz, L, _ = x.shape
            xz = x @ in_proj_w.T
            xi, z = jnp.split(xz, 2, axis=-1)
            xc = xi.transpose(0, 2, 1)
            xc = lax.conv_general_dilated(xc, conv_w, window_strides=(1,), padding=[(D_CONV - 1, 0)], feature_group_count=D_INNER, dimension_numbers=('NCH', 'OIH', 'NCH'))
            xc = xc + conv_b[None, :, None]
            xc = jax.nn.silu(xc).transpose(0, 2, 1)
            x_dbl = xc @ x_proj_w.T
            dt, Bmat, Cmat = jnp.split(x_dbl, [DT_RANK, DT_RANK + D_STATE], axis=-1)
            dt = jax.nn.softplus(dt @ dt_proj_w.T + dt_proj_b)
            A = -jnp.exp(A_log)
            dA = jnp.exp(dt[..., None] * A)
            dBx = dt[..., None] * Bmat[:, :, None, :] * xc[..., None]

            def step(h, inp):
                dA_t, dBx_t, C_t = inp
                h = dA_t * h + dBx_t
                y = jnp.einsum('bdn,bn->bd', h, C_t)
                return (h, y)
            h0 = jnp.zeros((Bsz, D_INNER, D_STATE), x.dtype)
            _, ys = lax.scan(step, h0, (dA.transpose(1, 0, 2, 3), dBx.transpose(1, 0, 2, 3), Cmat.transpose(1, 0, 2)))
            y = ys.transpose(1, 0, 2)
            y = y + D * xc
            y = y * jax.nn.silu(z)
            return y @ out_proj_w.T
        x = x + _mamba(_layernorm(x, ln1_g, ln1_b), in_proj_w, conv_w, conv_b, x_proj_w, dt_proj_w, dt_proj_b, A_log, D, out_proj_w)
        h = _layernorm(x, ln2_g, ln2_b)
        f = jax.nn.relu(h @ ffn_w1.T + ffn_b1) @ ffn_w2.T + ffn_b2
        return x + f

    def _L0_ffn_ref(hidden_states, Wg, Wu, Wd):
        import jax, jax.numpy as jnp
        import numpy as np
        NUM_EXPERTS = 8
        HIDDEN = 128
        FFN = 512
        BATCH = 2
        SEQ = 256
        B, S, H = hidden_states.shape
        x = hidden_states.reshape(-1, H)

        def expert_step(acc, w):
            wg, wu, wd = w
            h = jax.nn.silu(x @ wg) * (x @ wu)
            return (acc + h @ wd, None)
        acc, _ = jax.lax.scan(expert_step, jnp.zeros_like(x), (Wg, Wu, Wd))
        return acc.reshape(B, S, H)
    x = L0_attn_x
    x = _layernorm(x + _L0_attn_ref(x, L0_attn_in_proj_w, L0_attn_conv_w, L0_attn_conv_b, L0_attn_x_proj_w, L0_attn_dt_proj_w, L0_attn_dt_proj_b, L0_attn_A_log, L0_attn_D, L0_attn_out_proj_w, L0_attn_ln1_g, L0_attn_ln1_b, L0_attn_ln2_g, L0_attn_ln2_b, L0_attn_ffn_w1, L0_attn_ffn_b1, L0_attn_ffn_w2, L0_attn_ffn_b2), axis=-1)
    x = _layernorm(x + _L0_ffn_ref(x, L0_ffn_Wg, L0_ffn_Wu, L0_ffn_Wd), axis=-1)
    return x

_drawn_inputs = setup_inputs


def setup_inputs(seed=0):
    import zlib

    import numpy as np

    out = dict(_drawn_inputs(seed))
    spreads = {'L0_attn_dt_proj_b': (-4.600166320800781, 0.6),
     'L0_attn_D': (1.0, 0.6),
     'L0_attn_ln1_g': (1.0, 0.6),
     'L0_attn_ln1_b': (0.0, 0.8),
     'L0_attn_ln2_g': (1.0, 0.6),
     'L0_attn_ln2_b': (0.0, 2.0),
     'L0_attn_ffn_b1': (0.0, 2.0),
     'L0_attn_ffn_b2': (0.0, 2.0)}
    factors = {'L0_attn_in_proj_w': 8.0,
     'L0_attn_conv_w': 8.0,
     'L0_attn_conv_b': 8.0,
     'L0_attn_x_proj_w': 8.0,
     'L0_attn_dt_proj_w': 8.0,
     'L0_attn_A_log': 8.0,
     'L0_attn_out_proj_w': 8.0,
     'L0_attn_ffn_w1': 64.0,
     'L0_attn_ffn_w2': 63.289}
    for name, (base, spread) in spreads.items():
        noise = np.random.default_rng([zlib.crc32(name.encode()), seed]).standard_normal(out[name].shape)
        drawn = base * np.exp(spread * noise) if base else spread * noise
        out[name] = jnp.asarray(drawn.astype(out[name].dtype))
    for name, factor in factors.items():
        out[name] = (out[name] * factor).astype(out[name].dtype)
    return out
```

```python
from contextlib import ExitStack

import concourse.bass as bass
from concourse import mybir

F32 = mybir.dt.float32
F32R = mybir.dt.float32r
ALU = mybir.AluOpType
ACT = mybir.ActivationFunctionType

P = 128
EPS = 1e-5
DMA = 16

PACK = {}
_at = 0
for _name, _n in (("g1", 1), ("b1", 1), ("g2", 1), ("b2", 1), ("conv_w", 8), ("conv_b", 2),
                  ("dt_b", 2), ("D", 2), ("ffn_b1", 4), ("A_log", 32)):
    PACK[_name] = (_at, _at + _n)
    _at += _n
PACKED = _at


def build(nc, x, packed, win, xproj, dtproj, wout, w1, w2, ffn_b2, wg, wu, wd, out):
    B, L, DM = x.shape
    NE, _, FF = wg.shape
    NS = 16
    TOK = 512
    NCH = B * L // TOK
    NJ = TOK // P
    NB = TOK // L
    DI = win.shape[1] // 2
    NT = DI // P
    TAPS = 4
    FT = FF // P
    UNITS = NE * FT
    HALF = UNITS // 2
    FFT = w1.shape[1] // P
    SLOTS = UNITS
    DA_RING, W_RING, GU_RING, SG_RING, HM_RING = 8, 2, 2, 2, 4
    BURST = 4
    assert SLOTS == 2 * NS and DM == P and DA_RING == 2 * BURST
    BC = 2 * NS
    DTR = dtproj.shape[0]
    DT0 = 2 * BC
    XP = DT0 + DTR

    x_view = x.rearrange("(c b) (h p) d -> c p (b h) d", b=NB, p=P)
    out_view = out.rearrange("(c b) (h p) d -> c p (b h) d", b=NB, p=P)

    with ExitStack() as ctx:
        def sb(name, shape, dt=F32):
            return ctx.enter_context(nc.sbuf_tensor(name, shape, dt))

        def ps(name, shape):
            return ctx.enter_context(nc.psum_tensor(name, shape, F32))

        def sem(name):
            return ctx.enter_context(nc.semaphore(name))

        par = sb("par", [P, PACKED])
        a_neg = sb("a_neg", [P, NT, NS])
        win_sb = sb("win_sb", [P, 2 * DI])
        xproj_sb = sb("xproj_sb", [P, NT, XP])
        dtproj_sb = sb("dtproj_sb", [XP, DI])
        wout_sb = sb("wout_sb", [P, NT, DM])
        w1_sb = sb("w1_sb", [P, FFT * P])
        w2_sb = sb("w2_sb", [P, FFT, DM])
        b2_rows = sb("b2_rows", [P, DM])
        wg_hi = sb("wg_hi", [P, NE, FF], F32R)
        wg_lo = sb("wg_lo", [P, NE, FF], F32R)
        wu_hi = sb("wu_hi", [P, NE, FF], F32R)
        wu_lo = sb("wu_lo", [P, NE, FF], F32R)
        wd_sb = sb("wd_sb", [P, NE, FT, DM])
        w_stage = sb("w_stage", [P, 2, FF])
        ident = sb("ident", [P, P])
        ident_r = sb("ident_r", [P, P], F32R)
        pick = sb("pick", [2 * BC, BC])
        pick_r = sb("pick_r", [2 * BC, BC], F32R)
        minus_half = sb("minus_half", [P, NJ])

        xf = sb("xf", [P, NJ, DM])
        xn1 = sb("xn1", [P, NJ, DM])
        xnT = sb("xnT", [P, TOK])
        xi = sb("xi", [P, NT, NB, L + TAPS - 1])
        xc = sb("xc", [P, NT, TOK])
        bcdt = sb("bcdt", [XP, TOK])
        sp_relu = sb("sp_relu", [P, NT, TOK])
        sz = sb("sz", [P, NT, TOK])
        bc = sb("bc", [2 * BC, TOK], F32R)
        dt = sb("dt", [P, NT, TOK])
        u = sb("u", [P, NT, TOK])
        b_rep = sb("b_rep", [P, 2, TOK])
        dA = sb("dA", [P, DA_RING, NT, NB, L])
        w = sb("w", [P, W_RING, NT, TOK])
        h = sb("h", [P, NT, TOK])
        y = sb("y", [P, NT, TOK])
        y2 = sb("y2", [P, NT, TOK])
        xb = sb("xb", [P, NJ, DM])
        x1 = sb("x1", [P, NJ, DM])
        xn2 = sb("xn2", [P, NJ, DM])
        hT = sb("hT", [P, TOK])
        fh = sb("fh", [P, FFT, TOK])
        sp_exp = fh[:, 0:NT, :]
        sp_log = fh[:, NT:2 * NT, :]
        x_hi = sb("x_hi", [P, TOK], F32R)
        x_lo = sb("x_lo", [P, TOK], F32R)
        sg = sb("sg", [P, SG_RING, TOK])
        hm = sb("hm", [P, HM_RING, TOK])
        yT = sb("yT", [P, TOK])
        res = sb("res", [P, NJ, DM])
        stats = sb("stats", [P, 4, NJ, 6])
        mv = sb("mv", [P, 4, NJ, 2])
        ve = sb("ve", [P, 4, NJ])
        rstd = sb("rstd", [P, 4, NJ])

        ps_g = ps("ps_g", [P, GU_RING, TOK])
        ps_u = ps("ps_u", [P, GU_RING, TOK])
        ps_y = ps("ps_y", [P, TOK])
        ps_b = ps("ps_b", [P, TOK])
        ps_c = ps("ps_c", [P, TOK])
        ps_m = ps("ps_m", [P, TOK])

        def col(name, k=0):
            return par[:, PACK[name][0] + k:PACK[name][0] + k + 1]

        par_loaded, small_loaded, wd_loaded = sem("par_loaded"), sem("small_loaded"), sem("wd_loaded")
        stage_loaded, stage_hi, stage_lo = sem("stage_loaded"), sem("stage_hi"), sem("stage_lo")
        ident_steps, consts_made, a_exp, a_made = sem("ident_steps"), sem("consts_made"), sem("a_exp"), sem("a_made")
        ring_zeroed, pads_zeroed = sem("ring_zeroed"), sem("pads_zeroed")
        xf_loaded, xb_loaded, stored = sem("xf_loaded"), sem("xb_loaded"), sem("stored")
        ln_steps = [sem(f"ln_steps{k}") for k in range(4)]
        ln_var = [sem(f"ln_var{k}") for k in range(4)]
        ln_rstd = [sem(f"ln_rstd{k}") for k in range(4)]
        ln_done = [sem(f"ln_done{k}") for k in range(4)]
        aggr_held = sem("aggr_held")
        m_full, m_free = sem("m_full"), sem("m_free")
        xi_ready = sem("xi_ready")
        conv_taps = sem("conv_taps")
        xc_ready = sem("xc_ready")
        sp_abs = sem("sp_abs")
        sp_exps = sem("sp_exps")
        sp_logs = sem("sp_logs")
        sp_rest = sem("sp_rest")
        sp_round = sem("sp_round")
        dt_ready, u_ready = sem("dt_ready"), sem("u_ready")
        bc_hi, bc_lo = sem("bc_hi"), sem("bc_lo")
        b_spread, c_spread, b_copied = sem("b_spread"), sem("c_spread"), sem("b_copied")
        dA_ready, w_ready = sem("dA_ready"), sem("w_ready")
        scanned, read_out, y_added = sem("scanned"), sem("read_out"), sem("y_added")
        y_begun = sem("y_begun")
        y2_ready = sem("y2_ready")
        x1_ready = sem("x1_ready")
        x_hi_ready = sem("x_hi_ready")
        gu_full, silu_ready, hm_ready, down_done = (
            sem("gu_full"), sem("silu_ready"), sem("hm_ready"), sem("down_done"))
        yT_ready = sem("yT_ready")

        def wait(eng, s, value):
            if not (isinstance(value, int) and value <= 0):
                eng.wait_ge(s, value)

        def has(i, off):
            return not isinstance(i, int) or 0 <= i + off < NCH

        M_USES = [(0, "z0", 0), (1, "z1", 0), (2, "out_proj", -1), (3, "turn1", 1), (4, "xi0", 1),
                  (5, "turn2", -1), (6, "ffn1_0", -1), (7, "ffn1_1", -1), (8, "ffn1_2", -1),
                  (9, "ffn1_3", -1), (10, "xi1", 1), (11, "ffn2", -1), (13, "x_proj", 1),
                  (14, "turn3", -1), (16, "dt0", 1), (17, "dt1", 1), (20, "turn4", -2)]
        LOOP0, LOOP1 = 2, NCH - 1

        def m_count(i, name):
            if not isinstance(i, int):
                return m_count(LOOP0, name) + (i - LOOP0) * len(M_USES)
            before = sum(has(j, off) for j in range(-1, i) for _, _, off in M_USES)
            names = [n for _, n, off in M_USES if has(i, off)]
            return before + names.index(name) + 1

        ITER = list(range(-1, NCH + 2))

        def pipeline(eng, body):
            for i in ITER:
                if i < LOOP0 or i >= LOOP1:
                    body(i)
                elif i == LOOP0:
                    with eng.Fori(LOOP0, LOOP1) as r:
                        body(r)

        N_STAGE = 2 * NE // 2

        block = ctx.enter_context(nc.Block())

        @block.sync
        def _(sp):
            sp.dma_start(xf[:, :, :], x_view[0, :, :, :]).then_inc(xf_loaded, DMA)
            sp.dma_start(par[:, :], packed).then_inc(par_loaded, DMA)
            sp.dma_start(win_sb[:, :], win).then_inc(small_loaded, DMA)
            sp.dma_start(xproj_sb[:, :, :], xproj.rearrange("(k p) n -> p k n", p=P)).then_inc(small_loaded, DMA)
            sp.dma_start(dtproj_sb[DT0:XP, :], dtproj).then_inc(small_loaded, DMA)
            sp.dma_start(wout_sb[:, :, :], wout.rearrange("(k p) n -> p k n", p=P)).then_inc(small_loaded, DMA)
            sp.dma_start(w1_sb[:, :], w1).then_inc(small_loaded, DMA)
            sp.dma_start(w2_sb[:, :, :], w2.rearrange("(k p) n -> p k n", p=P)).then_inc(small_loaded, DMA)
            sp.dma_start(b2_rows[:, :], ffn_b2).then_inc(small_loaded, DMA)
            for s in range(N_STAGE):
                src = (wg, wu)[s // (NE // 2)]
                e = 2 * (s % (NE // 2))
                wait(sp, stage_lo, s)
                sp.dma_start(w_stage[:, :, :], src[e:e + 2, :, :].rearrange("e p f -> p e f")).then_inc(stage_loaded, DMA)
                if s == 1:
                    sp.dma_start(wd_sb[:, :, :, :], wd.rearrange("e (k p) d -> p e k d", p=P)).then_inc(wd_loaded, DMA)

            def body(i):
                if has(i, 2):
                    wait(sp, ln_done[0], i + 2)
                    sp.dma_start(xf[:, :, :], x_view[bass.ds(i + 2, 1), :, :, :].rearrange("c p j d -> p (c j) d")).then_inc(xf_loaded, DMA)
                if has(i, -1):
                    wait(sp, x1_ready, 3 * (i - 1))
                    sp.dma_start(xb[:, :, :], x_view[bass.ds(i - 1, 1), :, :, :].rearrange("c p j d -> p (c j) d")).then_inc(xb_loaded, DMA)
                if has(i, -2):
                    sp.wait_ge(m_free, m_count(i, "turn4"))
                    sp.dma_start(out_view[bass.ds(i - 2, 1), :, :, :].rearrange("c p j d -> p (c j) d"), res[:, :, :]).then_inc(stored, DMA)

            for i in ITER:
                if i < LOOP0 or i >= LOOP1 - 1:
                    body(i)
                elif i == LOOP0:
                    with sp.Fori(LOOP0, LOOP1 - 1) as r:
                        body(r)
            sp.wait_ge(stored, DMA * NCH)

        @block.tensor
        def _(pe):
            mm = nc.tensor.matmul

            def m_begin(i, name):
                wait(pe, m_free, m_count(i, name) - 1)

            def turn(dst, src):
                for j in range(NJ):
                    last = nc.tensor.transpose(dst[:, j * P:(j + 1) * P], src[:, j * P:(j + 1) * P], ident[:, :])
                return last

            def spread(c, n):
                g = c * NS + n
                if n == 0:
                    wait(pe, bc_lo, c + 1)
                wait(pe, b_copied, g)
                mm(ps_b[:, :], pick_r[:, n:n + 1].to_broadcast([2 * BC, P]), bc[:, :],
                   start=True, stop=True).then_inc(b_spread, 1)
                wait(pe, read_out, g)
                mm(ps_c[:, :], pick_r[:, NS + n:NS + n + 1].to_broadcast([2 * BC, P]), bc[:, :],
                   start=True, stop=True).then_inc(c_spread, 1)

            def up(c, k):
                e, f = divmod(k, FT)
                r = k % GU_RING
                g = c * UNITS + k
                if k == 0:
                    wait(pe, m_free, m_count(c + 1, "turn3"))
                if isinstance(c, int) and c == 0 and f == 0 and e % 2 == 0:
                    pe.wait_ge(stage_lo, N_STAGE)
                wait(pe, hm_ready, g - GU_RING + 1)
                for bank, hi, lo in ((ps_g, wg_hi, wg_lo), (ps_u, wu_hi, wu_lo)):
                    cols = slice(f * P, (f + 1) * P)
                    mm(bank[:, r, :], hi[:, e, cols], x_hi[:, :], start=True, stop=False)
                    mm(bank[:, r, :], hi[:, e, cols], x_lo[:, :], start=False, stop=False)
                    last = mm(bank[:, r, :], lo[:, e, cols], x_hi[:, :], start=False, stop=True)
                last.then_inc(gu_full, 1)

            def down(c, k):
                e, f = divmod(k, FT)
                if k == 0:
                    wait(pe, yT_ready, c)
                    if isinstance(c, int) and c == 0:
                        pe.wait_ge(wd_loaded, DMA)
                    mm(ps_y[:, :], ident_r[:, :], x_hi[:, :], start=True, stop=False)
                    mm(ps_y[:, :], ident_r[:, :], x_lo[:, :], start=False, stop=False)
                wait(pe, hm_ready, c * UNITS + k + 1)
                mm(ps_y[:, :], wd_sb[:, e, f, :], hm[:, k % HM_RING, :], start=False,
                   stop=(k == UNITS - 1)).then_inc(down_done, 1)

            def misc(i, name):
                m_begin(i, name)
                if name in ("z0", "z1"):
                    t = int(name[1])
                    mm(ps_m[:, :], win_sb[:, DI + t * P:DI + (t + 1) * P], xnT[:, :],
                       start=True, stop=True).then_inc(m_full, 1)
                elif name in ("xi0", "xi1"):
                    if name == "xi0":
                        wait(pe, m_free, m_count(i, "turn1"))
                    t = int(name[2])
                    mm(ps_m[:, :], win_sb[:, t * P:(t + 1) * P], xnT[:, :],
                       start=True, stop=True).then_inc(m_full, 1)
                elif name == "turn1":
                    wait(pe, ln_done[0], i + 2)
                    turn(ps_m, xn1[:, :, :].rearrange("p j d -> p (j d)")).then_inc(m_full, 1)
                elif name == "x_proj":
                    wait(pe, xc_ready, 2 * (i + 2))
                    for t in range(NT):
                        last = mm(ps_m[0:XP, :], xproj_sb[:, t, :], xc[:, t, :], start=(t == 0), stop=(t == NT - 1))
                    last.then_inc(m_full, 1)
                elif name in ("dt0", "dt1"):
                    t = int(name[2])
                    wait(pe, m_free, m_count(i, "x_proj"))
                    mm(ps_m[:, :], dtproj_sb[DT0:XP, t * P:(t + 1) * P], bcdt[DT0:XP, :],
                       start=True, stop=True).then_inc(m_full, 1)
                elif name == "out_proj":
                    wait(pe, y2_ready, i)
                    for j in range(NJ):
                        for t in range(NT):
                            last = mm(ps_m[:, j * P:(j + 1) * P], y2[:, t, j * P:(j + 1) * P], wout_sb[:, t, :],
                                      start=(t == 0), stop=(t == NT - 1))
                    last.then_inc(m_full, 1)
                elif name in ("turn2", "turn3"):
                    k = int(name[4]) - 1
                    wait(pe, ln_done[k], i)
                    turn(ps_m, xn2[:, :, :].rearrange("p j d -> p (j d)")).then_inc(m_full, 1)
                elif name.startswith("ffn1_"):
                    t = int(name[5])
                    wait(pe, m_free, m_count(i, "turn2"))
                    mm(ps_m[:, :], w1_sb[:, t * P:(t + 1) * P], hT[:, :], start=True, stop=True).then_inc(m_full, 1)
                elif name == "ffn2":
                    wait(pe, m_free, m_count(i, "ffn1_3"))
                    for j in range(NJ):
                        for t in range(FFT):
                            last = mm(ps_m[:, j * P:(j + 1) * P], fh[:, t, j * P:(j + 1) * P], w2_sb[:, t, :],
                                      start=(t == 0), stop=(t == FFT - 1))
                    last.then_inc(m_full, 1)
                elif name == "turn4":
                    wait(pe, yT_ready, i - 1)
                    turn(ps_m, yT[:, :]).then_inc(m_full, 1)

            def body(i):
                for k in range(SLOTS):
                    uo, uk = (-2, HALF + k) if k < HALF else (-1, k - HALF)
                    if has(i, uo):
                        up(i + uo, uk)
                    if k % 2 == 1 and k < SLOTS - 1 and has(i, 0):
                        spread(i, (k + 1) // 2)
                    if k == SLOTS - 1 and has(i, 1):
                        spread(i + 1, 0)
                    for slot, name, off in M_USES:
                        if slot == k and has(i, off):
                            misc(i, name)
                    do, dk = (-2, HALF + k - 2) if k < HALF + 2 else (-1, k - HALF - 2)
                    if has(i, do):
                        down(i + do, dk)

            pe.wait_ge(consts_made, 3)
            pe.wait_ge(small_loaded, 7 * DMA)
            pipeline(pe, body)

        @block.scalar
        def _(act):
            fn = nc.scalar.activation

            def m_wait(i, name):
                act.wait_ge(m_full, m_count(i, name))

            def exps(c, n):
                g = c * NS + n
                wait(act, scanned, g - DA_RING + 1)
                for t in range(NT):
                    last = fn(dA[:, n % DA_RING, t, :, 1:L],
                              dt[:, t, :].rearrange("p (b l) -> p b l", b=NB)[:, :, 1:L],
                              ACT.Exp, scale=a_neg[:, t, n:n + 1])
                last.then_inc(dA_ready, 1)

            def burst(i, q):
                c, n0 = (i, (q + 1) * BURST) if q < 3 else (i + 1, 0)
                if q == 3:
                    wait(act, dt_ready, i + 2)
                for n in range(n0, n0 + BURST):
                    exps(c, n)

            def softplus_logs(i):
                act.wait_ge(sp_abs, 2 * (i + 2))
                fn(sp_exp, sp_exp, ACT.Exp, scale=-1.0).then_inc(sp_exps, 1)
                act.wait_ge(sp_exps, i + 2)
                fn(sp_log, sp_exp, ACT.Ln, bias=1.0).then_inc(sp_logs, 1)

            def silu(c, k):
                g = c * UNITS + k
                act.wait_ge(gu_full, g + 1)
                wait(act, hm_ready, g - SG_RING + 1)
                fn(sg[:, k % SG_RING, :], ps_g[:, k % GU_RING, :], ACT.Silu).then_inc(silu_ready, 1)

            def copy_b(c, n):
                g = c * NS + n
                act.wait_ge(b_spread, g + 1)
                wait(act, w_ready, g - 1)
                fn(b_rep[:, n % 2, :], ps_b[:, :], ACT.Copy).then_inc(b_copied, 1)

            def begin_y(i):
                wait(act, y2_ready, i)
                for t in range(NT):
                    fn(y[:, t, :], xc[:, t, :], ACT.Copy, scale=col("D", t)).then_inc(y_begun, 1)

            def misc(i, name):
                m_wait(i, name)
                if name in ("z0", "z1"):
                    t = int(name[1])
                    wait(act, y2_ready, i)
                    fn(sz[:, t, :], ps_m[:, :], ACT.Silu).then_inc(m_free, 1)
                elif name == "turn1":
                    fn(xnT[:, :], ps_m[:, :], ACT.Identity, scale=col("g1"), bias=col("b1")).then_inc(m_free, 1)
                elif name in ("xi0", "xi1"):
                    t = int(name[2])
                    wait(act, sp_rest, 2 * (i + 1))
                    wait(act, u_ready, i + 1)
                    v = ps_m[:, :].rearrange("p (b l) -> p b l", b=NB)
                    fn(xi[:, t, :, TAPS - 1:], v, ACT.Copy).then_inc(xi_ready, 1)
                    fn(xc[:, t, :].rearrange("p (b l) -> p b l", b=NB), v, ACT.Copy,
                       scale=col("conv_w", TAPS * t + TAPS - 1)).then_inc(m_free, 1)
                elif name == "x_proj":
                    wait(act, bc_lo, i + 1)
                    fn(bcdt[:, :], ps_m[0:XP, :], ACT.Copy).then_inc(m_free, 1)
                elif name in ("dt0", "dt1"):
                    t = int(name[2])
                    if t == 0:
                        wait(act, dt_ready, i + 1)
                        if has(i, -1):
                            wait(act, m_full, m_count(i, "ffn2"))
                    fn(sp_exp[:, t, :], ps_m[:, :], ACT.Abs, bias=col("dt_b", t)).then_inc(sp_abs, 1)
                    fn(sp_relu[:, t, :], ps_m[:, :], ACT.Relu, bias=col("dt_b", t)).then_inc(m_free, 1)
                elif name == "turn2":
                    fn(hT[:, :], ps_m[:, :], ACT.Identity, scale=col("g2"), bias=col("b2")).then_inc(m_free, 1)
                elif name.startswith("ffn1_"):
                    t = int(name[5])
                    if t == 0 and has(i, 0):
                        wait(act, dt_ready, i + 1)
                    fn(fh[:, t, :], ps_m[:, :], ACT.Relu, bias=col("ffn_b1", t)).then_inc(m_free, 1)
                elif name == "turn3":
                    wait(act, gu_full, UNITS * (i - 1))
                    fn(x_hi[:, :], ps_m[:, :], ACT.Copy).then_inc(x_hi_ready, 1)

            def conv_silu(i, t):
                act.wait_ge(conv_taps, (TAPS - 1) * (2 * (i + 1) + t + 1))
                fn(xc[:, t, :], xc[:, t, :], ACT.Silu, bias=col("conv_b", t)).then_inc(xc_ready, 1)

            def body(i):
                for k in range(SLOTS):
                    if k == 1 and has(i, 0):
                        begin_y(i)
                    q, at = divmod(k, 8)
                    if at == 3 and has(i, 0 if q < 3 else 1):
                        burst(i, q)
                    if k == 19 and has(i, 1):
                        softplus_logs(i)
                    if k == HALF + 2 and has(i, -2):
                        act.wait_ge(down_done, UNITS * (i - 1))
                        fn(yT[:, :], ps_y[:, :], ACT.Copy).then_inc(yT_ready, 1)
                    uo, uk = (-2, HALF + k) if k < HALF else (-1, k - HALF)
                    if has(i, uo):
                        silu(i + uo, uk)
                    if k % 2 == 1 and k < SLOTS - 1 and has(i, 0):
                        copy_b(i, (k + 1) // 2)
                    if k == SLOTS - 1 and has(i, 1):
                        copy_b(i + 1, 0)
                    for slot, name, off in M_USES:
                        if slot == k and has(i, off) and name not in ("out_proj", "ffn2", "turn4"):
                            misc(i, name)
                    if k in (5, 12) and has(i, 1):
                        conv_silu(i, 0 if k == 5 else 1)

            act.wait_ge(par_loaded, DMA)
            lo, hi = PACK["A_log"]
            fn(a_neg[:, :, :].rearrange("p t n -> p (t n)"), par[:, lo:hi], ACT.Exp).then_inc(a_exp, 1)
            act.wait_ge(a_made, 1)
            act.wait_ge(ring_zeroed, 1)
            act.wait_ge(pads_zeroed, 1)
            body(-1)
            for s in range(N_STAGE):
                dst = (wg_hi, wu_hi)[s // (NE // 2)]
                e = 2 * (s % (NE // 2))
                act.wait_ge(stage_loaded, DMA * (s + 1))
                fn(dst[:, e:e + 2, :], w_stage[:, :, :], ACT.Copy).then_inc(stage_hi, 1)
            for i in ITER[1:]:
                if i < LOOP0 or i >= LOOP1:
                    body(i)
                elif i == LOOP0:
                    with act.Fori(LOOP0, LOOP1) as r:
                        body(r)

        @block.vector
        def _(dve):
            tt, ts, stt = nc.vector.tensor_tensor, nc.vector.tensor_scalar, nc.vector.scalar_tensor_tensor

            def ln_stats(k, c, src):
                for j in range(NJ):
                    last = nc.vector.bn_stats(stats[:, k, j, :], src[:, j * P:(j + 1) * P])
                last.then_inc(ln_steps[k], 1)
                dve.wait_ge(ln_steps[k], 2 * c + 1)
                dve.sem_inc(aggr_held, 1)
                for j in range(NJ):
                    last = nc.vector.bn_aggr(mv[:, k, j, :], stats[:, k, j, :])
                last.then_inc(ln_steps[k], 1)
                dve.wait_ge(ln_steps[k], 2 * c + 2)
                ts(ve[:, k, :], mv[:, k, :, 1], EPS, None, ALU.add).then_inc(ln_var[k], 1)

            def ln_norm(k, c, dst, src):
                dve.wait_ge(ln_rstd[k], c + 1)
                for j in range(NJ):
                    last = ts(dst[:, j, :], src[:, j * P:(j + 1) * P], mv[:, k, j, 0:1], rstd[:, k, j:j + 1],
                              ALU.subtract, ALU.mult)
                return last

            def flat(tile):
                return tile[:, :, :].rearrange("p j d -> p (j d)")

            def scan(i, n):
                g = i * NS + n
                dve.wait_ge(dA_ready, g + 1)
                dve.wait_ge(w_ready, g + 1)
                wait(dve, y_added, g)
                nc.vector.tensor_tensor_scan(
                    flat(h), dA[:, n % DA_RING, :, :, :].rearrange("p t b l -> p (t b l)"),
                    w[:, n % W_RING, :, :].rearrange("p t l -> p (t l)"), 0.0, ALU.mult, ALU.add).then_inc(scanned, 1)
                dve.wait_ge(scanned, g + 1)
                dve.wait_ge(c_spread, g + 1)
                tt(h[:, :, :], h[:, :, :], ps_c[:, :].unsqueeze(1).to_broadcast([P, NT, TOK]), ALU.mult).then_inc(read_out, 1)
                dve.wait_ge(read_out, g + 1)
                if n == 0:
                    dve.wait_ge(y_begun, 2 * (i + 1))
                tt(y[:, :, :], y[:, :, :], h[:, :, :], ALU.add).then_inc(y_added, 1)

            def gate(i):
                dve.wait_ge(y_added, NS * i)
                dve.wait_ge(m_free, m_count(i - 1, "z1"))
                tt(y2[:, :, :], y[:, :, :], sz[:, :, :], ALU.mult).then_inc(y2_ready, 1)

            def residual1(i):
                dve.wait_ge(xb_loaded, DMA * i)
                dve.wait_ge(m_full, m_count(i, "out_proj"))
                tt(flat(x1), flat(xb), ps_m[:, :], ALU.add).then_inc(m_free, 1)
                dve.wait_ge(m_free, m_count(i, "out_proj"))
                ln_stats(1, i - 1, flat(x1))

            def residual2(i):
                tt(flat(x1), flat(x1), flat(xb), ALU.add).then_inc(x1_ready, 1)
                dve.wait_ge(x1_ready, 3 * (i - 1) + 1)
                tt(x1[:, :, :], x1[:, :, :], b2_rows[:, :].unsqueeze(1).to_broadcast([P, NJ, DM]), ALU.add).then_inc(x1_ready, 2)

            def residual3(i):
                dve.wait_ge(x1_ready, 3 * i)
                dve.wait_ge(m_full, m_count(i, "ffn2"))
                tt(flat(x1), flat(x1), ps_m[:, :], ALU.add).then_inc(m_free, 1)
                dve.wait_ge(m_free, m_count(i, "ffn2"))
                ln_stats(2, i - 1, flat(x1))

            def conv(i, t):
                dve.wait_ge(m_free, m_count(i, f"xi{t}"))
                acc = xc[:, t, :].rearrange("p (b l) -> p b l", b=NB)
                for k in range(TAPS - 1):
                    if k:
                        dve.wait_ge(conv_taps, (TAPS - 1) * (2 * (i + 1) + t) + k)
                    stt(acc, xi[:, t, :, k:k + L], col("conv_w", TAPS * t + k), acc,
                        ALU.mult, ALU.add).then_inc(conv_taps, 1)

            def times(c, k):
                g = c * UNITS + k
                dve.wait_ge(silu_ready, g + 1)
                wait(dve, down_done, g - HM_RING + 1)
                tt(hm[:, k % HM_RING, :], sg[:, k % SG_RING, :], ps_u[:, k % GU_RING, :], ALU.mult).then_inc(hm_ready, 1)

            def split_bc(i):
                dve.wait_ge(m_free, m_count(i, "x_proj"))
                wait(dve, c_spread, NS * (i + 1))
                nc.vector.tensor_copy(bc[:, :], bcdt[0:2 * BC, :]).then_inc(bc_hi, 1)
                dve.wait_ge(bc_hi, i + 2)
                tt(bc[BC:2 * BC, :], bcdt[BC:2 * BC, :], bc[BC:2 * BC, :].bitcast(F32), ALU.subtract).then_inc(bc_lo, 1)

            def body(i):
                for k in range(SLOTS):
                    if k == 0 and has(i, -1):
                        gate(i)
                    if k == 1 and has(i, 1):
                        dve.wait_ge(xf_loaded, DMA * (i + 2))
                        ln_stats(0, i + 1, flat(xf))
                    if k == 2 and has(i, 1):
                        if has(i, 0):
                            dve.wait_ge(m_full, m_count(i - 1, "turn1"))
                        ln_norm(0, i + 1, xn1, flat(xf)).then_inc(ln_done[0], 1)
                    if k == 3 and has(i, -1):
                        residual1(i)
                    if k == 4 and has(i, -1):
                        ln_norm(1, i - 1, xn2, flat(x1)).then_inc(ln_done[1], 1)
                    if k == 5 and has(i, 1):
                        conv(i, 0)
                    if k == 7 and has(i, -1):
                        residual2(i)
                    if k == 11 and has(i, 1):
                        conv(i, 1)
                    if k == 12 and has(i, -1):
                        residual3(i)
                    if k == 13 and has(i, -1):
                        ln_norm(2, i - 1, xn2, flat(x1)).then_inc(ln_done[2], 1)
                    if k == 15 and has(i, -1):
                        dve.wait_ge(x_hi_ready, i)
                        tt(x_lo[:, :], ps_m[:, :], x_hi[:, :].bitcast(F32), ALU.subtract).then_inc(m_free, 1)
                    if k == 20 and has(i, 1):
                        dve.wait_ge(sp_exps, i + 2)
                        ts(xi[:, :, :, TAPS - 1:], sp_exp.rearrange("p t (b l) -> p t b l", b=NB), 1.0, -1.0,
                           ALU.add, ALU.add).then_inc(sp_round, 1)
                    if k == 22 and has(i, -2):
                        dve.wait_ge(m_full, m_count(i, "turn4"))
                        ln_stats(3, i - 2, ps_m[:, :])
                    if k == 23 and has(i, -2):
                        wait(dve, stored, DMA * (i - 2))
                        ln_norm(3, i - 2, res, ps_m[:, :]).then_inc(m_free, 1)
                    if k == SLOTS - 2 and has(i, 1):
                        split_bc(i)
                    if k % 2 == 0 and has(i, 0):
                        scan(i, k // 2)
                    uo, uk = (-2, HALF + k) if k < HALF else (-1, k - HALF)
                    if has(i, uo):
                        times(i + uo, uk)

            nc.vector.memset(dA[:, :, :, :, 0:1], 0.0).then_inc(ring_zeroed, 1)
            nc.vector.memset(xi[:, :, :, 0:TAPS - 1], 0.0).then_inc(pads_zeroed, 1)
            dve.wait_ge(a_exp, 1)
            ts(a_neg[:, :, :], a_neg[:, :, :], -1.0, None, ALU.mult).then_inc(a_made, 1)
            pipeline(dve, body)

        @block.gpsimd
        def _(pool):
            tt = nc.gpsimd.tensor_tensor

            def rsqrt(k, c):
                pool.wait_ge(ln_var[k], c + 1)
                tt(rstd[:, k, :], ve[:, k, :], minus_half[:, :], ALU.pow).then_inc(ln_rstd[k], 1)

            def dbx(c, n):
                g = c * NS + n
                pool.wait_ge(b_copied, g + 1)
                wait(pool, scanned, g - W_RING + 1)
                if n == 0:
                    pool.wait_ge(u_ready, c + 1)
                tt(w[:, n % W_RING, :, :], u[:, :, :], b_rep[:, n % 2, :].unsqueeze(1).to_broadcast([P, NT, TOK]),
                   ALU.mult).then_inc(w_ready, 1)

            def softplus_sum(i):
                e = sp_exp.rearrange("p t (b l) -> p t b l", b=NB)
                pool.wait_ge(sp_round, i + 2)
                pool.wait_ge(sp_logs, i + 2)
                tt(e, e, xi[:, :, :, TAPS - 1:], ALU.subtract).then_inc(sp_rest, 1)
                pool.wait_ge(sp_rest, 2 * (i + 1) + 1)
                tt(sp_log, sp_log, sp_exp, ALU.add).then_inc(sp_rest, 1)
                pool.wait_ge(sp_rest, 2 * (i + 2))
                pool.wait_ge(m_free, m_count(i, "dt1"))
                wait(pool, dA_ready, NS * (i + 1))
                tt(dt[:, :, :], sp_relu[:, :, :], sp_log, ALU.add).then_inc(dt_ready, 1)

            def body(i):
                for k in range(SLOTS):
                    for ln, slot, off in ((0, 1, 1), (1, 3, -1), (2, 12, -1), (3, 22, -2)):
                        if k == slot and has(i, off):
                            rsqrt(ln, i + off)
                    if k % 2 == 1 and k < SLOTS - 1 and has(i, 0):
                        dbx(i, (k + 1) // 2)
                    if k == 20 and has(i, 1):
                        softplus_sum(i)
                    if k == SLOTS - 1 and has(i, 1):
                        pool.wait_ge(dt_ready, i + 2)
                        wait(pool, w_ready, NS * (i + 1))
                        tt(u[:, :, :], dt[:, :, :], xc[:, :, :], ALU.mult).then_inc(u_ready, 1)
                        dbx(i + 1, 0)

            nc.gpsimd.memset(minus_half[:, :], -0.5).then_inc(ident_steps, 1)
            nc.gpsimd.memset(ident[:, :], 0.0).then_inc(ident_steps, 1)
            nc.gpsimd.memset(pick[:, :], 0.0).then_inc(ident_steps, 1)
            pool.wait_ge(ident_steps, 3)
            nc.gpsimd.affine_select(out=ident[:, :], in_=ident[:, :], compare_op=ALU.not_equal, fill=1.0,
                                    base=0, pattern=[[-1, P]], channel_multiplier=1).then_inc(consts_made, 1)
            for part in range(2):
                nc.gpsimd.affine_select(out=pick[:, :], in_=pick[:, :], compare_op=ALU.not_equal, fill=1.0,
                                        base=-part * BC, pattern=[[-1, BC]], channel_multiplier=1).then_inc(ident_steps, 1)
                pool.wait_ge(ident_steps, 4 + part)
            pool.wait_ge(consts_made, 1)
            nc.gpsimd.tensor_copy(ident_r[:, :], ident[:, :]).then_inc(consts_made, 1)
            nc.gpsimd.tensor_copy(pick_r[:, :], pick[:, :]).then_inc(consts_made, 1)
            body(-1)
            for s in range(N_STAGE):
                hi, lo = ((wg_hi, wg_lo), (wu_hi, wu_lo))[s // (NE // 2)]
                e = 2 * (s % (NE // 2))
                pool.wait_ge(stage_hi, s + 1)
                tt(lo[:, e:e + 2, :], w_stage[:, :, :], hi[:, e:e + 2, :].bitcast(F32), ALU.subtract).then_inc(stage_lo, 1)
            for i in ITER[1:]:
                if i < LOOP0 or i >= LOOP1:
                    body(i)
                elif i == LOOP0:
                    with pool.Fori(LOOP0, LOOP1) as r:
                        body(r)


def kernel(L0_attn_x, L0_attn_in_proj_w, L0_attn_conv_w, L0_attn_conv_b, L0_attn_x_proj_w, L0_attn_dt_proj_w,
           L0_attn_dt_proj_b, L0_attn_A_log, L0_attn_D, L0_attn_out_proj_w, L0_attn_ln1_g, L0_attn_ln1_b,
           L0_attn_ln2_g, L0_attn_ln2_b, L0_attn_ffn_w1, L0_attn_ffn_b1, L0_attn_ffn_w2, L0_attn_ffn_b2,
           L0_ffn_Wg, L0_ffn_Wu, L0_ffn_Wd):
    import numpy as np
    import concourse.bacc as bacc
    from concourse.bass_utils import run_bass_kernel_spmd

    def channels(a, tail=1):
        a = np.asarray(a).reshape(-1, P, tail)
        return a.transpose(1, 0, 2).reshape(P, -1)

    parts = {
        "g1": channels(L0_attn_ln1_g), "b1": channels(L0_attn_ln1_b),
        "g2": channels(L0_attn_ln2_g), "b2": channels(L0_attn_ln2_b),
        "conv_w": channels(L0_attn_conv_w, 4), "conv_b": channels(L0_attn_conv_b),
        "dt_b": channels(L0_attn_dt_proj_b), "D": channels(L0_attn_D),
        "ffn_b1": channels(L0_attn_ffn_b1), "A_log": channels(L0_attn_A_log, 16),
    }
    xp = np.asarray(L0_attn_x_proj_w)
    rank = np.asarray(L0_attn_dt_proj_w).shape[1]
    arrays = {
        "x": np.asarray(L0_attn_x),
        "packed": np.concatenate([parts[k] for k in PACK], axis=1),
        "win": np.asarray(L0_attn_in_proj_w).T,
        "xproj": np.concatenate([xp[rank:], xp[rank:], xp[:rank]], axis=0).T,
        "dtproj": np.asarray(L0_attn_dt_proj_w).T,
        "wout": np.asarray(L0_attn_out_proj_w).T,
        "w1": np.asarray(L0_attn_ffn_w1).T,
        "w2": np.asarray(L0_attn_ffn_w2).T,
        "ffn_b2": np.broadcast_to(np.asarray(L0_attn_ffn_b2), (P, P)),
        "wg": np.asarray(L0_ffn_Wg), "wu": np.asarray(L0_ffn_Wu), "wd": np.asarray(L0_ffn_Wd),
    }
    arrays = {k: np.ascontiguousarray(v) for k, v in arrays.items()}
    nc = bacc.Bacc("TRN2", target_bir_lowering=False, num_devices=1, dynamic_dma_scratch_size=1024)
    args = {k: nc.dram_tensor(k, v.shape, mybir.dt.from_np(v.dtype), kind="ExternalInput").ap()
            for k, v in arrays.items()}
    out = nc.dram_tensor("out", arrays["x"].shape, F32, kind="ExternalOutput").ap()
    build(nc, **args, out=out)
    r = run_bass_kernel_spmd(nc, [arrays], core_ids=[0])
    return r.results[0]["out"]
```

```python
from contextlib import ExitStack

import concourse.bass as bass
from concourse import mybir

F32 = mybir.dt.float32
F32R = mybir.dt.float32r
ALU = mybir.AluOpType
ACT = mybir.ActivationFunctionType

P = 128
EPS = 1e-5
DMA = 16

PACK = {}
_at = 0
for _name, _n in (("g1", 1), ("b1", 1), ("g2", 1), ("b2", 1), ("conv_w", 8), ("conv_b", 2),
                  ("dt_b", 2), ("D", 2), ("ffn_b1", 4), ("A_log", 32)):
    PACK[_name] = (_at, _at + _n)
    _at += _n
PACKED = _at


def build(nc, x, packed, win, xproj, dtproj, wout, w1, w2, ffn_b2, wg, wu, wd, out):
    B, L, DM = x.shape
    NE, _, FF = wg.shape
    NS = 16
    TOK = 512
    NCH = B * L // TOK
    NJ = TOK // P
    NB = TOK // L
    DI = win.shape[1] // 2
    NT = DI // P
    TAPS = 4
    FT = FF // P
    UNITS = NE * FT
    FFT = w1.shape[1] // P
    SLOTS = UNITS
    SWITCH = 20
    DA_RING, W_RING, GU_RING, SG_RING, HM_RING = 8, 2, 2, 2, 8
    BURST = 4
    POOL_ADDS = (2, 3, 6, 7, 10, 11)
    BURST_AT = (4, 12, 20, 28)
    assert SLOTS == 2 * NS and DM == P and DA_RING == 2 * BURST
    BC = 2 * NS
    DTR = dtproj.shape[0]
    DT0 = 2 * BC
    XP = DT0 + DTR

    x_view = x.rearrange("(c b) (h p) d -> c p (b h) d", b=NB, p=P)
    out_view = out.rearrange("(c b) (h p) d -> c p (b h) d", b=NB, p=P)

    with ExitStack() as ctx:
        def sb(name, shape, dt=F32):
            return ctx.enter_context(nc.sbuf_tensor(name, shape, dt))

        def ps(name, shape):
            return ctx.enter_context(nc.psum_tensor(name, shape, F32))

        def sem(name):
            return ctx.enter_context(nc.semaphore(name))

        par = sb("par", [P, PACKED])
        a_neg = sb("a_neg", [P, NT, NS])
        win_sb = sb("win_sb", [P, 2 * DI])
        xproj_sb = sb("xproj_sb", [P, NT, XP])
        dtproj_sb = sb("dtproj_sb", [XP, DI])
        wout_sb = sb("wout_sb", [P, NT, DM])
        w1_sb = sb("w1_sb", [P, FFT * P])
        w2_sb = sb("w2_sb", [P, FFT, DM])
        b2_rows = sb("b2_rows", [P, DM])
        wg_hi = sb("wg_hi", [P, NE, FF], F32R)
        wg_lo = sb("wg_lo", [P, NE, FF], F32R)
        wu_hi = sb("wu_hi", [P, NE, FF], F32R)
        wu_lo = sb("wu_lo", [P, NE, FF], F32R)
        wd_sb = sb("wd_sb", [P, NE, FT, DM])
        ident = sb("ident", [P, P])
        ident_r = sb("ident_r", [P, P], F32R)
        pick = sb("pick", [2 * BC, BC])
        pick_r = sb("pick_r", [2 * BC, BC], F32R)
        minus_half = sb("minus_half", [P, NJ])
        one = sb("one", [P, 1])

        xf = sb("xf", [P, NJ, DM])
        xn1_hT = sb("xn1_hT", [P, TOK])
        xn1 = xn1_hT[:, :].rearrange("p (j d) -> p j d", d=DM)
        hT = xn1_hT
        xnT = sb("xnT", [P, TOK])
        xi = sb("xi", [P, NT, NB, L + TAPS - 1])
        xc = sb("xc", [P, NT, TOK])
        bcdt = sb("bcdt", [XP, TOK])
        sp_relu = sb("sp_relu", [P, NT, TOK])
        sz = sb("sz", [P, NT, TOK])
        bc = sb("bc", [2 * BC, TOK], F32R)
        bc_late = sb("bc_late", [2 * BC, TOK], F32R)
        dt = sb("dt", [P, NT, TOK])
        u = sb("u", [P, NT, TOK])
        b_rep = sb("b_rep", [P, 2, TOK])
        dA = sb("dA", [P, DA_RING, NT, NB, L])
        w = sb("w", [P, W_RING, NT, TOK])
        h = sb("h", [P, NT, TOK])
        y = sb("y", [P, NT, TOK])
        xb = sb("xb", [P, NJ, DM])
        x1 = sb("x1", [P, NJ, DM])
        xn2 = sb("xn2", [P, NJ, DM])
        fh = sb("fh", [P, FFT, TOK])
        sp_exp = fh[:, 0:NT, :]
        sp_log = fh[:, NT:2 * NT, :]
        y2 = fh[:, 0:NT, :]
        x_hi = sb("x_hi", [P, TOK], F32R)
        x_lo = sb("x_lo", [P, TOK], F32R)
        sg = sb("sg", [P, SG_RING, TOK])
        hm = sb("hm", [P, HM_RING, TOK])
        yT = xn2[:, :, :].rearrange("p j d -> p (j d)")
        w_stage = hm[:, :, :].rearrange("p (r e) f -> p r e f", e=2)
        res = sb("res", [P, NJ, DM])
        stats = sb("stats", [P, 4, NJ, 6])
        mv = sb("mv", [P, 4, NJ, 2])
        ve = sb("ve", [P, 4, NJ])
        rstd = sb("rstd", [P, 4, NJ])

        ps_g = ps("ps_g", [P, GU_RING, TOK])
        ps_u = ps("ps_u", [P, GU_RING, TOK])
        ps_y = ps("ps_y", [P, TOK])
        ps_b = ps("ps_b", [P, TOK])
        ps_c = ps("ps_c", [P, TOK])
        ps_m = ps("ps_m", [P, TOK])

        def col(name, k=0):
            return par[:, PACK[name][0] + k:PACK[name][0] + k + 1]

        par_loaded, small_loaded, wd_loaded = sem("par_loaded"), sem("small_loaded"), sem("wd_loaded")
        stage_loaded = [sem(f"stage_loaded{r}") for r in range(HM_RING // 2)]
        stage_hi, stage_lo = sem("stage_hi"), sem("stage_lo")
        ident_steps, consts_made, halves_made, a_exp, a_made = sem("ident_steps"), sem("consts_made"), sem("halves_made"), sem("a_exp"), sem("a_made")
        ring_zeroed, pads_zeroed = sem("ring_zeroed"), sem("pads_zeroed")
        xf_loaded, xb_loaded, stored = sem("xf_loaded"), sem("xb_loaded"), sem("stored")
        ln_steps = [sem(f"ln_steps{k}") for k in range(4)]
        ln_var = [sem(f"ln_var{k}") for k in range(4)]
        ln_rstd = [sem(f"ln_rstd{k}") for k in range(4)]
        ln_done = [sem(f"ln_done{k}") for k in range(4)]
        aggr_held = sem("aggr_held")
        m_full, m_free = sem("m_full"), sem("m_free")
        xi_ready = sem("xi_ready")
        conv_taps = sem("conv_taps")
        xc_ready = sem("xc_ready")
        sp_abs = sem("sp_abs")
        sp_exps = sem("sp_exps")
        sp_logs = sem("sp_logs")
        sp_rest = sem("sp_rest")
        sp_round = sem("sp_round")
        dt_ready, u_ready = sem("dt_ready"), sem("u_ready")
        bc_hi, bc_lo, bc_kept = sem("bc_hi"), sem("bc_lo"), sem("bc_kept")
        b_spread, c_spread, b_copied = sem("b_spread"), sem("c_spread"), sem("b_copied")
        dA_ready, w_ready = sem("dA_ready"), sem("w_ready")
        scanned, read_out, y_added = sem("scanned"), sem("read_out"), sem("y_added")
        y_begun = sem("y_begun")
        y2_ready = sem("y2_ready")
        x1_ready = sem("x1_ready")
        x_hi_ready = sem("x_hi_ready")
        gu_full, silu_ready, hm_ready, down_done = (
            sem("gu_full"), sem("silu_ready"), sem("hm_ready"), sem("down_done"))
        yT_ready = sem("yT_ready")

        def wait(eng, s, value):
            if not (isinstance(value, int) and value <= 0):
                eng.wait_ge(s, value)

        def has(i, off):
            return not isinstance(i, int) or 0 <= i + off < NCH

        M_USES = [(1, "z0", 0), (2, "z1", 0), (3, "turn1", 1), (4, "out_proj", -1), (5, "xi0", 1),
                  (7, "xi1", 1), (8, "turn2", -1), (9, "ffn1_0", -1), (10, "ffn1_1", -1), (11, "ffn1_2", -1),
                  (12, "ffn1_3", -1), (15, "ffn2", -1), (16, "x_proj", 1), (17, "dt0", 1), (18, "dt1", 1),
                  (19, "turn3", -1), (24, "turn4", -2)]
        LOOP0, LOOP1 = 2, NCH - 2

        def m_count(i, name):
            if not isinstance(i, int):
                return m_count(LOOP0, name) + (i - LOOP0) * len(M_USES)
            before = sum(has(j, off) for j in range(-1, i) for _, _, off in M_USES)
            names = [n for _, n, off in M_USES if has(i, off)]
            return before + names.index(name) + 1

        def add_to_y(eng, tt, i, n):
            g = i * NS + n
            eng.wait_ge(read_out, g + 1)
            if n == 0:
                eng.wait_ge(y_begun, 2 * (i + 1))
            wait(eng, y_added, g)
            tt(y[:, :, :], y[:, :, :], w[:, n % W_RING, :, :], ALU.add).then_inc(y_added, 1)

        ITER = list(range(-1, NCH + 2))

        def pipeline(eng, body):
            for i in ITER:
                if i < LOOP0 or i >= LOOP1:
                    body(i)
                elif i == LOOP0:
                    with eng.Fori(LOOP0, LOOP1) as r:
                        body(r)

        N_STAGE = 2 * NE // 2
        STAGE_RING = HM_RING // 2

        def stage_piece(i, k):
            at = {(0, 3 * p + 1): p for p in range(N_STAGE)}
            return at.get((i, k)) if isinstance(i, int) else None

        def unit_at(k):
            return (-2, UNITS - SWITCH + k) if k < SWITCH else (-1, k - SWITCH)

        def in_burst(k):
            return any(b <= k < b + 4 for b in BURST_AT)

        def c_state(k):
            if in_burst(k):
                return k // 2 if k in BURST_AT or k - 2 in BURST_AT else None
            return k // 2 if k % 2 == 1 else None

        def down_slot(j):
            burst = min(b for b in BURST_AT + (BURST_AT[0] + SLOTS,) if b > j)
            return burst + 2 if burst - j <= 3 else burst if burst - j <= 5 else j + 6

        block = ctx.enter_context(nc.Block())

        @block.sync
        def _(sp):
            sp.dma_start(xf[:, :, :], x_view[0, :, :, :]).then_inc(xf_loaded, DMA)
            sp.dma_start(par[:, :], packed).then_inc(par_loaded, DMA)
            sp.dma_start(win_sb[:, :], win).then_inc(small_loaded, DMA)
            sp.dma_start(xproj_sb[:, :, :], xproj.rearrange("(k p) n -> p k n", p=P)).then_inc(small_loaded, DMA)
            sp.dma_start(dtproj_sb[DT0:XP, :], dtproj).then_inc(small_loaded, DMA)
            sp.dma_start(wout_sb[:, :, :], wout.rearrange("(k p) n -> p k n", p=P)).then_inc(small_loaded, DMA)
            sp.dma_start(w1_sb[:, :], w1).then_inc(small_loaded, DMA)
            sp.dma_start(w2_sb[:, :, :], w2.rearrange("(k p) n -> p k n", p=P)).then_inc(small_loaded, DMA)
            sp.dma_start(b2_rows[:, :], ffn_b2).then_inc(small_loaded, DMA)
            def load_piece(s):
                src = (wg, wu)[s // (NE // 2)]
                e = 2 * (s % (NE // 2))
                wait(sp, stage_lo, s - STAGE_RING + 1)
                sp.dma_start(w_stage[:, s % STAGE_RING, :, :], src[e:e + 2, :, :].rearrange("e p f -> p e f")).then_inc(stage_loaded[s % STAGE_RING], DMA)

            for s in range(STAGE_RING):
                load_piece(s)
            sp.wait_ge(ln_done[0], 1)
            sp.dma_start(xf[:, :, :], x_view[1, :, :, :]).then_inc(xf_loaded, DMA)
            sp.dma_start(wd_sb[:, :, :, :], wd.rearrange("e (k p) d -> p e k d", p=P)).then_inc(wd_loaded, DMA)

            def body(i):
                if has(i, -1):
                    wait(sp, x1_ready, 3 * (i - 1))
                    sp.dma_start(xb[:, :, :], x_view[bass.ds(i - 1, 1), :, :, :].rearrange("c p j d -> p (c j) d")).then_inc(xb_loaded, DMA)
                if has(i, -2):
                    sp.wait_ge(m_free, m_count(i, "turn4"))
                    sp.dma_start(out_view[bass.ds(i - 2, 1), :, :, :].rearrange("c p j d -> p (c j) d"), res[:, :, :]).then_inc(stored, DMA)
                if has(i, 3):
                    wait(sp, ln_done[0], i + 3)
                    sp.dma_start(xf[:, :, :], x_view[bass.ds(i + 3, 1), :, :, :].rearrange("c p j d -> p (c j) d")).then_inc(xf_loaded, DMA)

            for i in ITER:
                if i < LOOP0 or i >= LOOP1 - 1:
                    body(i)
                    if i == -1:
                        for s in range(STAGE_RING, N_STAGE):
                            load_piece(s)
                elif i == LOOP0:
                    with sp.Fori(LOOP0, LOOP1 - 1) as r:
                        body(r)
            sp.wait_ge(stored, DMA * NCH)

        @block.tensor
        def _(pe):
            mm = nc.tensor.matmul

            def m_begin(i, name):
                wait(pe, m_free, m_count(i, name) - 1)

            def turn(dst, src):
                for j in range(NJ):
                    last = nc.tensor.transpose(dst[:, j * P:(j + 1) * P], src[:, j * P:(j + 1) * P], ident[:, :])
                return last

            def spread_b(c, n):
                if n == 0:
                    wait(pe, bc_lo, c + 1)
                wait(pe, b_copied, c * NS + n)
                mm(ps_b[:, :], pick_r[:, n:n + 1].to_broadcast([2 * BC, P]), bc[:, :],
                   start=True, stop=True).then_inc(b_spread, 1)

            def spread_c(c, n):
                if n == 0:
                    wait(pe, bc_kept, c + 1)
                wait(pe, read_out, c * NS + n)
                mm(ps_c[:, :], pick_r[:, NS + n:NS + n + 1].to_broadcast([2 * BC, P]), bc_late[:, :],
                   start=True, stop=True).then_inc(c_spread, 1)

            def up(c, k):
                e, f = divmod(k, FT)
                r = k % GU_RING
                g = c * UNITS + k
                if k == 0:
                    wait(pe, m_free, m_count(c + 1, "turn3"))
                if isinstance(c, int) and c == 0 and f == 0 and e % 2 == 0:
                    pe.wait_ge(stage_lo, N_STAGE)
                wait(pe, hm_ready, g - GU_RING + 1)
                for bank, hi, lo in ((ps_g, wg_hi, wg_lo), (ps_u, wu_hi, wu_lo)):
                    cols = slice(f * P, (f + 1) * P)
                    mm(bank[:, r, :], hi[:, e, cols], x_hi[:, :], start=True, stop=False)
                    mm(bank[:, r, :], hi[:, e, cols], x_lo[:, :], start=False, stop=False)
                    last = mm(bank[:, r, :], lo[:, e, cols], x_hi[:, :], start=False, stop=True)
                last.then_inc(gu_full, 1)

            def down(c, k):
                e, f = divmod(k, FT)
                if k == 0:
                    wait(pe, yT_ready, c)
                    if isinstance(c, int) and c == 0:
                        pe.wait_ge(wd_loaded, DMA)
                    mm(ps_y[:, :], ident_r[:, :], x_hi[:, :], start=True, stop=False)
                    mm(ps_y[:, :], ident_r[:, :], x_lo[:, :], start=False, stop=False)
                wait(pe, hm_ready, c * UNITS + k + 1)
                mm(ps_y[:, :], wd_sb[:, e, f, :], hm[:, k % HM_RING, :], start=False,
                   stop=(k == UNITS - 1)).then_inc(down_done, 1)

            def misc(i, name):
                m_begin(i, name)
                if name in ("z0", "z1"):
                    t = int(name[1])
                    mm(ps_m[:, :], win_sb[:, DI + t * P:DI + (t + 1) * P], xnT[:, :],
                       start=True, stop=True).then_inc(m_full, 1)
                elif name in ("xi0", "xi1"):
                    if name == "xi0":
                        wait(pe, m_free, m_count(i, "turn1"))
                    t = int(name[2])
                    mm(ps_m[:, :], win_sb[:, t * P:(t + 1) * P], xnT[:, :],
                       start=True, stop=True).then_inc(m_full, 1)
                elif name == "turn1":
                    wait(pe, ln_done[0], i + 2)
                    turn(ps_m, xn1[:, :, :].rearrange("p j d -> p (j d)")).then_inc(m_full, 1)
                elif name == "x_proj":
                    wait(pe, xc_ready, 2 * (i + 2))
                    for t in range(NT):
                        last = mm(ps_m[0:XP, :], xproj_sb[:, t, :], xc[:, t, :], start=(t == 0), stop=(t == NT - 1))
                    last.then_inc(m_full, 1)
                elif name in ("dt0", "dt1"):
                    t = int(name[2])
                    wait(pe, m_free, m_count(i, "x_proj"))
                    mm(ps_m[:, :], dtproj_sb[DT0:XP, t * P:(t + 1) * P], bcdt[DT0:XP, :],
                       start=True, stop=True).then_inc(m_full, 1)
                elif name == "out_proj":
                    wait(pe, y2_ready, i)
                    for j in range(NJ):
                        for t in range(NT):
                            last = mm(ps_m[:, j * P:(j + 1) * P], y2[:, t, j * P:(j + 1) * P], wout_sb[:, t, :],
                                      start=(t == 0), stop=(t == NT - 1))
                    last.then_inc(m_full, 1)
                elif name in ("turn2", "turn3"):
                    k = int(name[4]) - 1
                    wait(pe, ln_done[k], i)
                    turn(ps_m, xn2[:, :, :].rearrange("p j d -> p (j d)")).then_inc(m_full, 1)
                elif name.startswith("ffn1_"):
                    t = int(name[5])
                    wait(pe, m_free, m_count(i, "turn2"))
                    mm(ps_m[:, :], w1_sb[:, t * P:(t + 1) * P], hT[:, :], start=True, stop=True).then_inc(m_full, 1)
                elif name == "ffn2":
                    wait(pe, m_free, m_count(i, "ffn1_3"))
                    for j in range(NJ):
                        for t in range(FFT):
                            last = mm(ps_m[:, j * P:(j + 1) * P], fh[:, t, j * P:(j + 1) * P], w2_sb[:, t, :],
                                      start=(t == 0), stop=(t == FFT - 1))
                    last.then_inc(m_full, 1)
                elif name == "turn4":
                    wait(pe, yT_ready, i - 1)
                    turn(ps_m, yT).then_inc(m_full, 1)

            def body(i):
                for k in range(SLOTS):
                    if k - 2 in BURST_AT and has(i, 0):
                        spread_c(i, c_state(k))
                    for j in range(k - SLOTS, k):
                        if j + SLOTS > 0 and (down_slot(j) if j >= 0 else down_slot(j + SLOTS) - SLOTS) == k:
                            off, unit = unit_at(j) if j >= 0 else (-2, j + SLOTS - SWITCH)
                            if has(i, off):
                                down(i + off, unit)
                    if k % 2 == 1:
                        c, n = divmod(k // 2 + 2, NS)
                        if has(i, c):
                            spread_b(i + c, n)
                    if k - 2 not in BURST_AT and has(i, 0) and c_state(k) is not None:
                        spread_c(i, c_state(k))
                    off, unit = unit_at(k)
                    if has(i, off):
                        up(i + off, unit)
                    for slot, name, off in M_USES:
                        if slot == k and has(i, off):
                            misc(i, name)

            pe.wait_ge(consts_made, 3)
            pe.wait_ge(small_loaded, 7 * DMA)
            pipeline(pe, body)

        @block.scalar
        def _(act):
            fn = nc.scalar.activation

            def m_wait(i, name):
                act.wait_ge(m_full, m_count(i, name))

            def exps(c, n):
                g = c * NS + n
                wait(act, scanned, g - DA_RING + 1)
                for t in range(NT):
                    last = fn(dA[:, n % DA_RING, t, :, 1:L],
                              dt[:, t, :].rearrange("p (b l) -> p b l", b=NB)[:, :, 1:L],
                              ACT.Exp, scale=a_neg[:, t, n:n + 1])
                last.then_inc(dA_ready, 1)

            def burst(i, q):
                c, n0 = (i, (q + 1) * BURST) if q < 3 else (i + 1, 0)
                if q == 3:
                    wait(act, dt_ready, i + 2)
                for n in range(n0, n0 + BURST):
                    exps(c, n)

            def softplus_exp(i):
                act.wait_ge(sp_abs, 2 * (i + 2))
                fn(sp_exp, sp_exp, ACT.Exp, scale=-1.0).then_inc(sp_exps, 1)

            def softplus_log(i):
                act.wait_ge(sp_exps, i + 2)
                fn(sp_log, sp_exp, ACT.Ln, bias=1.0).then_inc(sp_logs, 1)

            def silu(c, k):
                g = c * UNITS + k
                act.wait_ge(gu_full, g + 1)
                wait(act, hm_ready, g - SG_RING + 1)
                fn(sg[:, k % SG_RING, :], ps_g[:, k % GU_RING, :], ACT.Silu).then_inc(silu_ready, 1)

            def copy_b(c, n):
                g = c * NS + n
                act.wait_ge(b_spread, g + 1)
                wait(act, w_ready, g - 1)
                fn(b_rep[:, n % 2, :], ps_b[:, :], ACT.Copy).then_inc(b_copied, 1)

            def begin_y(i):
                wait(act, y2_ready, i)
                for t in range(NT):
                    fn(y[:, t, :], xc[:, t, :], ACT.Copy, scale=col("D", t)).then_inc(y_begun, 1)

            def misc(i, name):
                m_wait(i, name)
                if name in ("z0", "z1"):
                    t = int(name[1])
                    wait(act, y2_ready, i)
                    fn(sz[:, t, :], ps_m[:, :], ACT.Silu).then_inc(m_free, 1)
                elif name == "turn1":
                    fn(xnT[:, :], ps_m[:, :], ACT.Identity, scale=col("g1"), bias=col("b1")).then_inc(m_free, 1)
                elif name in ("xi0", "xi1"):
                    t = int(name[2])
                    wait(act, sp_rest, 2 * (i + 1))
                    wait(act, u_ready, i + 1)
                    v = ps_m[:, :].rearrange("p (b l) -> p b l", b=NB)
                    fn(xi[:, t, :, TAPS - 1:], v, ACT.Copy).then_inc(xi_ready, 1)
                    fn(xc[:, t, :].rearrange("p (b l) -> p b l", b=NB), v, ACT.Copy,
                       scale=col("conv_w", TAPS * t + TAPS - 1)).then_inc(m_free, 1)
                elif name == "x_proj":
                    wait(act, bc_lo, i + 1)
                    fn(bcdt[:, :], ps_m[0:XP, :], ACT.Copy).then_inc(m_free, 1)
                elif name in ("dt0", "dt1"):
                    t = int(name[2])
                    if t == 0:
                        wait(act, dt_ready, i + 1)
                        if has(i, -1):
                            wait(act, m_full, m_count(i, "ffn2"))
                    fn(sp_exp[:, t, :], ps_m[:, :], ACT.Abs, bias=col("dt_b", t)).then_inc(sp_abs, 1)
                    fn(sp_relu[:, t, :], ps_m[:, :], ACT.Relu, bias=col("dt_b", t)).then_inc(m_free, 1)
                elif name == "turn2":
                    fn(hT[:, :], ps_m[:, :], ACT.Identity, scale=col("g2"), bias=col("b2")).then_inc(m_free, 1)
                elif name.startswith("ffn1_"):
                    t = int(name[5])
                    if t == 0 and has(i, 0):
                        wait(act, dt_ready, i + 1)
                    fn(fh[:, t, :], ps_m[:, :], ACT.Relu, bias=col("ffn_b1", t)).then_inc(m_free, 1)
                elif name == "turn3":
                    wait(act, gu_full, UNITS * (i - 1))
                    fn(x_hi[:, :], ps_m[:, :], ACT.Copy).then_inc(x_hi_ready, 1)

            def split_hi(s):
                dst = (wg_hi, wu_hi)[s // (NE // 2)]
                e = 2 * (s % (NE // 2))
                act.wait_ge(stage_loaded[s % STAGE_RING], DMA * (s // STAGE_RING + 1))
                fn(dst[:, e:e + 2, :], w_stage[:, s % STAGE_RING, :, :], ACT.Copy).then_inc(stage_hi, 1)

            def conv_silu(i, t):
                act.wait_ge(conv_taps, (TAPS - 1) * (2 * (i + 1) + t + 1))
                fn(xc[:, t, :], xc[:, t, :], ACT.Silu, bias=col("conv_b", t)).then_inc(xc_ready, 1)

            def body(i):
                for k in range(SLOTS):
                    if k % 2 == 1:
                        c, n = divmod(k // 2 + 2, NS)
                        if has(i, c):
                            copy_b(i + c, n)
                    if k == 1 and has(i, 0):
                        begin_y(i)
                    if k in BURST_AT:
                        q = BURST_AT.index(k)
                        if has(i, 0 if q < 3 else 1):
                            burst(i, q)
                        if q == 2 and has(i, 1):
                            softplus_exp(i)
                    if k == 23 and has(i, -2):
                        act.wait_ge(down_done, UNITS * (i - 1))
                        fn(yT, ps_y[:, :], ACT.Copy).then_inc(yT_ready, 1)
                    off, unit = unit_at(k)
                    if has(i, off):
                        silu(i + off, unit)
                    for slot, name, off in M_USES:
                        if slot == k and has(i, off) and name not in ("out_proj", "ffn2", "turn4"):
                            misc(i, name)
                    if k in (9, 11) and has(i, 1):
                        conv_silu(i, 0 if k == 9 else 1)
                    if k == 24 and has(i, 1):
                        softplus_log(i)
                    if stage_piece(i, k) is not None:
                        split_hi(stage_piece(i, k))

            act.wait_ge(par_loaded, DMA)
            lo, hi = PACK["A_log"]
            fn(a_neg[:, :, :].rearrange("p t n -> p (t n)"), par[:, lo:hi], ACT.Exp).then_inc(a_exp, 1)
            act.wait_ge(a_made, 1)
            act.wait_ge(ring_zeroed, 1)
            act.wait_ge(pads_zeroed, 1)
            pipeline(act, body)

        @block.vector
        def _(dve):
            tt, ts, stt = nc.vector.tensor_tensor, nc.vector.tensor_scalar, nc.vector.scalar_tensor_tensor

            def ln_stats(k, c, src):
                for j in range(NJ):
                    last = nc.vector.bn_stats(stats[:, k, j, :], src[:, j * P:(j + 1) * P])
                last.then_inc(ln_steps[k], 1)
                dve.wait_ge(ln_steps[k], 2 * c + 1)
                dve.sem_inc(aggr_held, 1)
                for j in range(NJ):
                    last = nc.vector.bn_aggr(mv[:, k, j, :], stats[:, k, j, :])
                last.then_inc(ln_steps[k], 1)
                dve.wait_ge(ln_steps[k], 2 * c + 2)
                ts(ve[:, k, :], mv[:, k, :, 1], EPS, None, ALU.add).then_inc(ln_var[k], 1)

            def ln_norm(k, c, dst, src):
                dve.wait_ge(ln_rstd[k], c + 1)
                for j in range(NJ):
                    last = ts(dst[:, j, :], src[:, j * P:(j + 1) * P], mv[:, k, j, 0:1], rstd[:, k, j:j + 1],
                              ALU.subtract, ALU.mult)
                return last

            def norm1(c):
                ln_norm(0, c, xn1, flat(xf)).then_inc(ln_done[0], 1)

            def flat(tile):
                return tile[:, :, :].rearrange("p j d -> p (j d)")

            def scan(i, n):
                g = i * NS + n
                dve.wait_ge(dA_ready, g + 1)
                dve.wait_ge(w_ready, g + 1)
                wait(dve, read_out, g)
                nc.vector.tensor_tensor_scan(
                    flat(h), dA[:, n % DA_RING, :, :, :].rearrange("p t b l -> p (t b l)"),
                    w[:, n % W_RING, :, :].rearrange("p t l -> p (t l)"), 0.0, ALU.mult, ALU.add).then_inc(scanned, 1)

            def read(i, n):
                g = i * NS + n
                dve.wait_ge(scanned, g + 1)
                dve.wait_ge(c_spread, g + 1)
                tt(w[:, n % W_RING, :, :], h[:, :, :], ps_c[:, :].unsqueeze(1).to_broadcast([P, NT, TOK]),
                   ALU.mult).then_inc(read_out, 1)
                if n not in POOL_ADDS:
                    add_to_y(dve, tt, i, n)

            def gate(i):
                dve.wait_ge(y_added, NS * i)
                dve.wait_ge(m_free, m_count(i - 1, "z1"))
                if has(i, 0):
                    dve.wait_ge(dt_ready, i + 1)
                tt(y2, y[:, :, :], sz[:, :, :], ALU.mult).then_inc(y2_ready, 1)

            def residual1(i):
                dve.wait_ge(xb_loaded, DMA * i)
                dve.wait_ge(m_full, m_count(i, "out_proj"))
                tt(flat(x1), flat(xb), ps_m[:, :], ALU.add).then_inc(m_free, 1)
                dve.wait_ge(m_free, m_count(i, "out_proj"))
                ln_stats(1, i - 1, flat(x1))

            def residual3(i):
                dve.wait_ge(x1_ready, 3 * i)
                dve.wait_ge(m_full, m_count(i, "ffn2"))
                tt(flat(x1), flat(x1), ps_m[:, :], ALU.add).then_inc(m_free, 1)
                dve.wait_ge(m_free, m_count(i, "ffn2"))
                ln_stats(2, i - 1, flat(x1))

            def conv(i, t):
                dve.wait_ge(m_free, m_count(i, f"xi{t}"))
                acc = xc[:, t, :].rearrange("p (b l) -> p b l", b=NB)
                for k in range(TAPS - 1):
                    if k:
                        dve.wait_ge(conv_taps, (TAPS - 1) * (2 * (i + 1) + t) + k)
                    stt(acc, xi[:, t, :, k:k + L], col("conv_w", TAPS * t + k), acc,
                        ALU.mult, ALU.add).then_inc(conv_taps, 1)

            def times(c, k):
                g = c * UNITS + k
                dve.wait_ge(silu_ready, g + 1)
                wait(dve, down_done, g - HM_RING + 1)
                tt(hm[:, k % HM_RING, :], sg[:, k % SG_RING, :], ps_u[:, k % GU_RING, :], ALU.mult).then_inc(hm_ready, 1)

            def split_bc(i):
                dve.wait_ge(m_free, m_count(i, "x_proj"))
                wait(dve, b_spread, NS * (i + 1))
                wait(dve, bc_kept, i + 1)
                nc.vector.tensor_copy(bc[:, :], bcdt[0:2 * BC, :]).then_inc(bc_hi, 1)
                dve.wait_ge(bc_hi, i + 2)
                tt(bc[BC:2 * BC, :], bcdt[BC:2 * BC, :], bc[BC:2 * BC, :].bitcast(F32), ALU.subtract).then_inc(bc_lo, 1)

            def body(i):
                for k in range(SLOTS):
                    if k == 0 and has(i, -1):
                        gate(i)
                    if k in BURST_AT and has(i, 0):
                        scan(i, k // 2)
                        read(i, k // 2)
                    if k == 4 and has(i, -1):
                        residual1(i)
                    if k in BURST_AT and has(i, 0):
                        scan(i, k // 2 + 1)
                    off, unit = unit_at(k)
                    if has(i, off):
                        times(i + off, unit)
                    if k == 19 and has(i, -1):
                        dve.wait_ge(x_hi_ready, i)
                        tt(x_lo[:, :], ps_m[:, :], x_hi[:, :].bitcast(F32), ALU.subtract).then_inc(m_free, 1)
                    if has(i, 0) and not in_burst(k):
                        (scan if k % 2 == 0 else read)(i, k // 2)
                    if has(i, 0) and k - 1 in BURST_AT:
                        read(i, k // 2 + 1)
                    if k == 6 and has(i, -1):
                        ln_norm(1, i - 1, xn2, flat(x1)).then_inc(ln_done[1], 1)
                    if k == 7 and has(i, 1):
                        conv(i, 0)
                    if k == 9 and has(i, 1):
                        conv(i, 1)
                    if k == 15 and has(i, -1):
                        residual3(i)
                    if k == 17 and has(i, -1):
                        ln_norm(2, i - 1, xn2, flat(x1)).then_inc(ln_done[2], 1)
                    if k == 22 and has(i, 1):
                        dve.wait_ge(sp_exps, i + 2)
                        ts(xi[:, :, :, TAPS - 1:], sp_exp.rearrange("p t (b l) -> p t b l", b=NB), 1.0, -1.0,
                           ALU.add, ALU.add).then_inc(sp_round, 1)
                    if k == 24 and has(i, -2):
                        dve.wait_ge(m_full, m_count(i, "turn4"))
                        ln_stats(3, i - 2, ps_m[:, :])
                    if k == 26 and has(i, -2):
                        wait(dve, stored, DMA * (i - 2))
                        ln_norm(3, i - 2, res, ps_m[:, :]).then_inc(m_free, 1)
                    if k == 26 and has(i, 2):
                        dve.wait_ge(xf_loaded, DMA * (i + 3))
                        ln_stats(0, i + 2, flat(xf))
                    if k == 27 and has(i, 1):
                        split_bc(i)
                    if k == 30 and has(i, 2):
                        dve.wait_ge(m_full, m_count(i, "turn1"))
                        if has(i, -1):
                            dve.wait_ge(m_full, m_count(i, "ffn1_3"))
                        norm1(i + 2)

            dve.wait_ge(xf_loaded, DMA)
            ln_stats(0, 0, flat(xf))
            norm1(0)
            nc.vector.memset(dA[:, :, :, :, 0:1], 0.0).then_inc(ring_zeroed, 1)
            nc.vector.memset(xi[:, :, :, 0:TAPS - 1], 0.0).then_inc(pads_zeroed, 1)
            dve.wait_ge(a_exp, 1)
            ts(a_neg[:, :, :], a_neg[:, :, :], -1.0, None, ALU.mult).then_inc(a_made, 1)
            pipeline(dve, body)

        @block.gpsimd
        def _(pool):
            tt = nc.gpsimd.tensor_tensor

            def rsqrt(k, c):
                pool.wait_ge(ln_var[k], c + 1)
                tt(rstd[:, k, :], ve[:, k, :], minus_half[:, :], ALU.pow).then_inc(ln_rstd[k], 1)

            def dbx(c, n):
                g = c * NS + n
                pool.wait_ge(b_copied, g + 1)
                wait(pool, y_added, g - W_RING + 1)
                if n == 0:
                    pool.wait_ge(u_ready, c + 1)
                tt(w[:, n % W_RING, :, :], u[:, :, :], b_rep[:, n % 2, :].unsqueeze(1).to_broadcast([P, NT, TOK]),
                   ALU.mult).then_inc(w_ready, 1)

            def softplus_sum(i, part):
                e = sp_exp.rearrange("p t (b l) -> p t b l", b=NB)
                if part == 0:
                    pool.wait_ge(sp_round, i + 2)
                    pool.wait_ge(sp_logs, i + 2)
                    tt(e, e, xi[:, :, :, TAPS - 1:], ALU.subtract).then_inc(sp_rest, 1)
                elif part == 1:
                    pool.wait_ge(sp_rest, 2 * (i + 1) + 1)
                    tt(sp_log, sp_log, sp_exp, ALU.add).then_inc(sp_rest, 1)
                else:
                    pool.wait_ge(sp_rest, 2 * (i + 2))
                    pool.wait_ge(m_free, m_count(i, "dt1"))
                    wait(pool, dA_ready, NS * (i + 1))
                    tt(dt[:, :, :], sp_relu[:, :, :], sp_log, ALU.add).then_inc(dt_ready, 1)

            def residual2(i):
                pool.wait_ge(ln_done[1], i)
                tt(x1[:, :, :], x1[:, :, :], xb[:, :, :], ALU.add).then_inc(x1_ready, 1)
                pool.wait_ge(x1_ready, 3 * (i - 1) + 1)
                tt(x1[:, :, :], x1[:, :, :], b2_rows[:, :].unsqueeze(1).to_broadcast([P, NJ, DM]), ALU.add).then_inc(x1_ready, 2)

            def scale_xc(i):
                pool.wait_ge(dt_ready, i + 2)
                wait(pool, w_ready, NS * (i + 1))
                tt(u[:, :, :], dt[:, :, :], xc[:, :, :], ALU.mult).then_inc(u_ready, 1)

            def keep_bc(i):
                pool.wait_ge(bc_lo, i + 2)
                wait(pool, c_spread, NS * (i + 1))
                tt(bc_late[:, :], bc[:, :].bitcast(F32), one[0:2 * BC, :].to_broadcast([2 * BC, TOK]), ALU.mult).then_inc(bc_kept, 1)

            def split_lo(s):
                hi, lo = ((wg_hi, wg_lo), (wu_hi, wu_lo))[s // (NE // 2)]
                e = 2 * (s % (NE // 2))
                pool.wait_ge(stage_hi, s + 1)
                tt(lo[:, e:e + 2, :], w_stage[:, s % STAGE_RING, :, :], hi[:, e:e + 2, :].bitcast(F32),
                   ALU.subtract).then_inc(stage_lo, 1)

            def body(i):
                for k in range(SLOTS):
                    for ln, slot, off in ((1, 5, -1), (2, 16, -1), (3, 25, -2), (0, 28, 2)):
                        if k == slot and has(i, off):
                            rsqrt(ln, i + off)
                    if k == 9 and has(i, -1):
                        residual2(i)
                    if k % 2 == 0 and has(i, 0) and k // 2 - 1 in POOL_ADDS:
                        add_to_y(pool, tt, i, k // 2 - 1)
                    if k % 2 == 0 and k < SLOTS - 2 and has(i, 0):
                        dbx(i, k // 2 + 1)
                    if k == SLOTS - 2 and has(i, 1):
                        dbx(i + 1, 0)
                    if k in (24, 25, 26) and has(i, 1):
                        softplus_sum(i, k - 24)
                    if k == SLOTS - 3 and has(i, 1):
                        scale_xc(i)
                    if k == SLOTS - 1 and has(i, 1):
                        keep_bc(i)
                    if stage_piece(i, k) is not None:
                        split_lo(stage_piece(i, k))

            nc.gpsimd.memset(minus_half[:, :], -0.5).then_inc(halves_made, 1)
            nc.gpsimd.memset(one[:, :], 1.0).then_inc(halves_made, 1)
            nc.gpsimd.memset(ident[:, :], 0.0).then_inc(ident_steps, 1)
            nc.gpsimd.memset(pick[:, :], 0.0).then_inc(ident_steps, 1)
            pool.wait_ge(ident_steps, 2)
            nc.gpsimd.affine_select(out=ident[:, :], in_=ident[:, :], compare_op=ALU.not_equal, fill=1.0,
                                    base=0, pattern=[[-1, P]], channel_multiplier=1).then_inc(consts_made, 1)
            for part in range(2):
                nc.gpsimd.affine_select(out=pick[:, :], in_=pick[:, :], compare_op=ALU.not_equal, fill=1.0,
                                        base=-part * BC, pattern=[[-1, BC]], channel_multiplier=1).then_inc(ident_steps, 1)
                pool.wait_ge(ident_steps, 3 + part)
            pool.wait_ge(consts_made, 1)
            pool.wait_ge(halves_made, 2)
            rsqrt(0, 0)
            nc.gpsimd.tensor_copy(ident_r[:, :], ident[:, :]).then_inc(consts_made, 1)
            nc.gpsimd.tensor_copy(pick_r[:, :], pick[:, :]).then_inc(consts_made, 1)
            pipeline(pool, body)


def kernel(L0_attn_x, L0_attn_in_proj_w, L0_attn_conv_w, L0_attn_conv_b, L0_attn_x_proj_w, L0_attn_dt_proj_w,
           L0_attn_dt_proj_b, L0_attn_A_log, L0_attn_D, L0_attn_out_proj_w, L0_attn_ln1_g, L0_attn_ln1_b,
           L0_attn_ln2_g, L0_attn_ln2_b, L0_attn_ffn_w1, L0_attn_ffn_b1, L0_attn_ffn_w2, L0_attn_ffn_b2,
           L0_ffn_Wg, L0_ffn_Wu, L0_ffn_Wd):
    import numpy as np
    import concourse.bacc as bacc
    from concourse.bass_utils import run_bass_kernel_spmd

    def channels(a, tail=1):
        a = np.asarray(a).reshape(-1, P, tail)
        return a.transpose(1, 0, 2).reshape(P, -1)

    parts = {
        "g1": channels(L0_attn_ln1_g), "b1": channels(L0_attn_ln1_b),
        "g2": channels(L0_attn_ln2_g), "b2": channels(L0_attn_ln2_b),
        "conv_w": channels(L0_attn_conv_w, 4), "conv_b": channels(L0_attn_conv_b),
        "dt_b": channels(L0_attn_dt_proj_b), "D": channels(L0_attn_D),
        "ffn_b1": channels(L0_attn_ffn_b1), "A_log": channels(L0_attn_A_log, 16),
    }
    xp = np.asarray(L0_attn_x_proj_w)
    rank = np.asarray(L0_attn_dt_proj_w).shape[1]
    arrays = {
        "x": np.asarray(L0_attn_x),
        "packed": np.concatenate([parts[k] for k in PACK], axis=1),
        "win": np.asarray(L0_attn_in_proj_w).T,
        "xproj": np.concatenate([xp[rank:], xp[rank:], xp[:rank]], axis=0).T,
        "dtproj": np.asarray(L0_attn_dt_proj_w).T,
        "wout": np.asarray(L0_attn_out_proj_w).T,
        "w1": np.asarray(L0_attn_ffn_w1).T,
        "w2": np.asarray(L0_attn_ffn_w2).T,
        "ffn_b2": np.broadcast_to(np.asarray(L0_attn_ffn_b2), (P, P)),
        "wg": np.asarray(L0_ffn_Wg), "wu": np.asarray(L0_ffn_Wu), "wd": np.asarray(L0_ffn_Wd),
    }
    arrays = {k: np.ascontiguousarray(v) for k, v in arrays.items()}
    nc = bacc.Bacc("TRN2", target_bir_lowering=False, num_devices=1, dynamic_dma_scratch_size=1024)
    args = {k: nc.dram_tensor(k, v.shape, mybir.dt.from_np(v.dtype), kind="ExternalInput").ap()
            for k, v in arrays.items()}
    out = nc.dram_tensor("out", arrays["x"].shape, F32, kind="ExternalOutput").ap()
    build(nc, **args, out=out)
    r = run_bass_kernel_spmd(nc, [arrays], core_ids=[0])
    return r.results[0]["out"]
```

```python
from contextlib import ExitStack

import concourse.bass as bass
from concourse import mybir

F32 = mybir.dt.float32
F32R = mybir.dt.float32r
ALU = mybir.AluOpType
ACT = mybir.ActivationFunctionType

P = 128
EPS = 1e-5
DMA = 16

PACK = {}
_at = 0
for _name, _n in (("g1", 1), ("b1", 1), ("g2", 1), ("b2", 1), ("conv_w", 8), ("conv_b", 2),
                  ("dt_b", 2), ("D", 2), ("ffn_b1", 4), ("A_log", 32)):
    PACK[_name] = (_at, _at + _n)
    _at += _n
PACKED = _at


def build(nc, x, packed, win, xproj, dtproj, wout, w1, w2, ffn_b2, wg, wu, wd, out):
    B, L, DM = x.shape
    NE, _, FF = wg.shape
    NS = 16
    TOK = 512
    NCH = B * L // TOK
    NJ = TOK // P
    NB = TOK // L
    DI = win.shape[1] // 2
    NT = DI // P
    TAPS = 4
    FT = FF // P
    UNITS = NE * FT
    FFT = w1.shape[1] // P
    SLOTS = UNITS
    DA_RING, W_RING, GU_RING, SG_RING, HM_RING = 8, 2, 2, 2, 8
    STAGE_RING = 3
    BURST = 4
    SWITCH = 20
    SPREAD_B_AT = (-2, -1.75, 2, 3, 3.75, 7.5, 9.25, 10.5, 12.5, 15.75, 17.5, 19.25, 21.5, 23.25, 25, 27.25)
    SPREAD_C_AT = (1, 3.25, 5.25, 7, 10.25, 12, 12.75, 14, 18, 19.25, 20.25, 21.25, 24, 27.75, 29.25, 30)
    DOWN_AT = (4, 4.5, 6, 6.25, 7.5, 8, 11.5, 11.5, 11.5, 12.5, 12.75, 13.5, 18, 20, 20, 20, 20.25, 20.5, 22,
               22.25, 25.75, 25.75, 27.75, 27.75, 28.25, 29.25, 29.5, 30, 31, 31.75, 34.25, 35.5)
    PE_AT = {"z0": 0.75, "z1": 2, "turn1": 3.25, "out_proj": 3.5, "xi0": 5.25, "xi1": 7.5, "turn2": 8.5,
             "ffn1_0": 10.25, "ffn1_1": 11, "ffn1_2": 12, "ffn1_3": 13.75, "ffn2": 16.25, "x_proj": 17,
             "dt0": 18.25, "dt1": 19, "turn3": 19.75, "turn4": 23.75}
    BURST_AT = (4, 11.5, 20.25, 28.25)
    COPY_B_AT = (-3.25, 0, 1, 2.5, 5.5, 7, 9.75, 11, 13.5, 15.25, 18.25, 18.75, 21.75, 23, 24.25, 26.75)
    ACT_AT = {"z0": 0.5, "begin_y": 0.75, "z1": 1.25, "turn1": 2.75, "xi0": 5.75, "norm2": 6, "xi1": 8,
              "turn2": 8.5, "conv_silu0": 9, "ffn1_0": 10, "conv_silu1": 10.5, "ffn1_1": 11, "ffn1_2": 11.5,
              "ffn1_3": 14.25, "x_proj": 16.75, "norm3": 17.5, "dt0": 17.75, "dt1": 18.5, "softplus_exp": 19.75,
              "turn3": 20, "yT": 22, "softplus_log": 26, "norm4": 29.5, "norm1": 31.25}
    SCAN_AT = (0.5, 1.5, 3.75, 6, 8.25, 10.25, 12, 14, 15, 17.75, 19, 19.75, 22.75, 25.75, 28.25, 29)
    READ_AT = (0.75, 3, 4, 6.25, 9.5, 11, 12, 14, 17, 18, 19.5, 20, 25.25, 27, 28.25, 29.5)
    POOL_ADDS = (0, 1, 2, 3, 6, 7, 9, 10, 15)
    ADD_AT = (2.75, 5, 5.75, 7, 9.75, 11.5, 11.75, 14, 17.25, 19.5, 21, 21.75, 26.25, 28, 28.25, 31.5)
    PE_SUMS = (1, 3, 4, 5, 6, 7, 9, 10, 11, 13, 14, 15)
    DVE_AT = {"gate": 0, "residual1": 3.75, "conv0": 6.75, "conv1": 8.75, "residual3": 15.75, "split_bc": 16.5,
              "x_lo": 19.25, "sp_round": 20.5, "stats4": 24, "stats1": 26.25}
    DBX_AT = (-0.5, 0, 2.75, 5.5, 6.5, 7, 10.75, 11.5, 12.5, 14, 17.5, 20.25, 21.75, 23.25, 28, 28.75)
    POOL_AT = {"rsqrt2": 5.5, "residual2": 10.25, "rsqrt3": 17, "sp_sum0": 23, "sp_sum1": 24, "sp_sum2": 25.25,
               "for_b": 28.5, "rsqrt4": 29.75, "scale_xc": 29.75, "rsqrt1": 30.75, "for_c": 31.25}
    STAGE_AT = ((-1, 2.75), (-1, 6.75), (-1, 14.75), (-1, 15), (-1, 16.25), (-1, 18), (0, 17.75), (1, 7.75))
    assert SLOTS == 2 * NS and DM == P and DA_RING == 2 * BURST
    BC = 2 * NS
    DTR = dtproj.shape[0]
    LO = xproj.shape[1] - BC - DTR
    XP = LO + BC + DTR
    assert LO >= BC + 2 * DTR and LO % 32 == 0

    x_view = x.rearrange("(c b) (h p) d -> c p (b h) d", b=NB, p=P)
    out_view = out.rearrange("(c b) (h p) d -> c p (b h) d", b=NB, p=P)

    with ExitStack() as ctx:
        def sb(name, shape, dt=F32):
            return ctx.enter_context(nc.sbuf_tensor(name, shape, dt))

        def ps(name, shape):
            return ctx.enter_context(nc.psum_tensor(name, shape, F32))

        def sem(name):
            return ctx.enter_context(nc.semaphore(name))

        par = sb("par", [P, PACKED])
        a_neg = sb("a_neg", [P, NT, NS])
        win_sb = sb("win_sb", [P, 2 * DI])
        xproj_sb = sb("xproj_sb", [P, NT, XP])
        dtproj_r = sb("dtproj_r", [XP, DI], F32R)
        wout_sb = sb("wout_sb", [P, NT, DM])
        w1_sb = sb("w1_sb", [P, FFT * P])
        w2_sb = sb("w2_sb", [P, FFT, DM])
        b2_rows = sb("b2_rows", [P, DM])
        wg_hi = sb("wg_hi", [P, NE, FF], F32R)
        wg_lo = sb("wg_lo", [P, NE, FF], F32R)
        wu_hi = sb("wu_hi", [P, NE, FF], F32R)
        wu_lo = sb("wu_lo", [P, NE, FF], F32R)
        wd_sb = sb("wd_sb", [P, NE, FT, DM])
        ident = sb("ident", [P, P])
        ident_r = sb("ident_r", [P, P], F32R)
        pick = sb("pick", [XP, BC])
        pick_r = sb("pick_r", [XP, BC], F32R)
        minus_half = sb("minus_half", [P, NJ])
        minus_one = sb("minus_one", [P, NJ])
        one = sb("one", [P, 1])

        xf = sb("xf", [P, NJ, DM])
        xn1_hT = sb("xn1_hT", [P, TOK])
        xn1 = xn1_hT[:, :].rearrange("p (j d) -> p j d", d=DM)
        hT = xn1_hT
        xnT = sb("xnT", [P, TOK])
        xi = sb("xi", [P, NT, NB, L + TAPS - 1])
        xc = sb("xc", [P, NT, TOK])
        bcdt = sb("bcdt", [XP, TOK])
        sp_relu = sb("sp_relu", [P, NT, TOK])
        sz = sb("sz", [P, NT, TOK])
        bc_new = sb("bc_new", [XP, TOK], F32R)
        bc = sb("bc", [XP, TOK], F32R)
        bc_late = sb("bc_late", [XP, TOK], F32R)
        dt = sb("dt", [P, NT, TOK])
        u = sb("u", [P, NT, TOK])
        b_rep = sb("b_rep", [P, 2, TOK])
        dA = sb("dA", [P, DA_RING, NT, NB, L])
        w = sb("w", [P, W_RING, NT, TOK])
        h = sb("h", [P, NT, TOK])
        y = sb("y", [P, NT, TOK])
        xb = sb("xb", [P, NJ, DM])
        x1 = sb("x1", [P, NJ, DM])
        xn2 = sb("xn2", [P, NJ, DM])
        fh = sb("fh", [P, FFT, TOK])
        sp_exp = fh[:, 0:NT, :]
        sp_log = fh[:, NT:2 * NT, :]
        y2 = fh[:, 0:NT, :]
        x_hi = sb("x_hi", [P, TOK], F32R)
        x_lo = sb("x_lo", [P, TOK], F32R)
        sg = sb("sg", [P, SG_RING, TOK])
        hm = sb("hm", [P, HM_RING, TOK])
        yT = xn2[:, :, :].rearrange("p j d -> p (j d)")
        w_stage = hm[:, 0:2 * STAGE_RING, :].rearrange("p (r e) f -> p r e f", e=2)
        hc0 = (sg, hm[:, 2 * STAGE_RING:, :])
        res = sb("res", [P, NJ, DM])
        dtw, dtw_hi, dtw_lo = sg[0:DTR, 0, 0:DI], x_hi[0:DTR, 0:DI], x_lo[0:DTR, 0:DI]
        stats = sb("stats", [P, 4, NJ, 6])
        mv = sb("mv", [P, 4, NJ, 2])
        ve = sb("ve", [P, 4, NJ])
        rstd = sb("rstd", [P, 4, NJ])
        minus_mean = sb("minus_mean", [P, 4, NJ])
        shift = sb("shift", [P, 4, NJ])

        ps_g = ps("ps_g", [P, GU_RING, TOK])
        ps_u = ps("ps_u", [P, GU_RING, TOK])
        ps_y = ps("ps_y", [P, TOK])
        ps_b = ps("ps_b", [P, TOK])
        ps_c = ps("ps_c", [P, TOK])
        ps_m = ps("ps_m", [P, TOK])

        def col(name, k=0):
            return par[:, PACK[name][0] + k:PACK[name][0] + k + 1]

        par_loaded, small_loaded, wd_loaded = sem("par_loaded"), sem("small_loaded"), sem("wd_loaded")
        stage_loaded = [sem(f"stage_loaded{r}") for r in range(STAGE_RING)]
        stage_hi, stage_lo = sem("stage_hi"), sem("stage_lo")
        ident_steps, consts_made, halves_made = sem("ident_steps"), sem("consts_made"), sem("halves_made")
        a_exp, a_made = sem("a_exp"), sem("a_made")
        dtw_loaded, dtw_steps, dtw_placed = sem("dtw_loaded"), sem("dtw_steps"), sem("dtw_placed")
        ring_zeroed, pads_zeroed = sem("ring_zeroed"), sem("pads_zeroed")
        xf_loaded, xb_loaded, stored = sem("xf_loaded"), sem("xb_loaded"), sem("stored")
        ln_steps = [sem(f"ln_steps{k}") for k in range(4)]
        ln_var = [sem(f"ln_var{k}") for k in range(4)]
        ln_rstd = [sem(f"ln_rstd{k}") for k in range(4)]
        ln_minus = [sem(f"ln_minus{k}") for k in range(4)]
        ln_shift = [sem(f"ln_shift{k}") for k in range(4)]
        ln_done = [sem(f"ln_done{k}") for k in range(4)]
        aggr_held = sem("aggr_held")
        m_full, m_free = sem("m_full"), sem("m_free")
        conv_taps = sem("conv_taps")
        xc_ready = sem("xc_ready")
        sp_abs = sem("sp_abs")
        sp_exps = sem("sp_exps")
        sp_logs = sem("sp_logs")
        sp_rest = sem("sp_rest")
        sp_round = sem("sp_round")
        dt_ready, u_ready = sem("dt_ready"), sem("u_ready")
        bc_hi, bc_lo, bc_for_b, bc_for_c = sem("bc_hi"), sem("bc_lo"), sem("bc_for_b"), sem("bc_for_c")
        b_spread, c_spread, b_copied = sem("b_spread"), sem("c_spread"), sem("b_copied")
        dA_ready, w_ready = sem("dA_ready"), sem("w_ready")
        scanned, read_out, y_added = sem("scanned"), sem("read_out"), sem("y_added")
        y_begun = sem("y_begun")
        y_folded = sem("y_folded")
        y2_ready = sem("y2_ready")
        x1_ready = sem("x1_ready")
        x_hi_ready = sem("x_hi_ready")
        gu_full, silu_ready, hm_ready, down_done = (
            sem("gu_full"), sem("silu_ready"), sem("hm_ready"), sem("down_done"))
        yT_ready = sem("yT_ready")

        def wait(eng, s, value):
            if not (isinstance(value, int) and value <= 0):
                eng.wait_ge(s, value)

        def has(i, off):
            return not isinstance(i, int) or 0 <= i + off < NCH

        def first(i):
            return isinstance(i, int) and i == -1

        USE_OFF = {"z0": 0, "z1": 0, "turn1": 1, "out_proj": -1, "xi0": 1, "xi1": 1, "turn2": -1,
                   "ffn1_0": -1, "ffn1_1": -1, "ffn1_2": -1, "ffn1_3": -1, "ffn2": -1, "x_proj": 1,
                   "dt0": 1, "dt1": 1, "turn3": -1, "turn4": -2}
        M_USES = [(name, USE_OFF[name]) for name in sorted(PE_AT, key=PE_AT.get)]
        LOOP0, LOOP1 = 2, NCH - 2

        def m_count(i, name):
            if not isinstance(i, int):
                return m_count(LOOP0, name) + (i - LOOP0) * len(M_USES)
            before = sum(has(j, off) for j in range(-1, i) for _, off in M_USES)
            names = [n for n, off in M_USES if has(i, off)]
            return before + names.index(name) + 1

        def softplus_sum(eng, tt, i, part):
            if part == 0:
                work = xi[:, :, :, TAPS - 1:]
                eng.wait_ge(sp_round, i + 2)
                tt(work, sp_exp.rearrange("p t (b l) -> p t b l", b=NB), work, ALU.subtract).then_inc(sp_rest, 1)
            elif part == 1:
                eng.wait_ge(sp_rest, 2 * (i + 1) + 1)
                eng.wait_ge(m_free, m_count(i, "dt1"))
                relu = sp_relu[:, :, :].rearrange("p t (b l) -> p t b l", b=NB)
                tt(relu, relu, xi[:, :, :, TAPS - 1:], ALU.add).then_inc(sp_rest, 1)
            else:
                eng.wait_ge(sp_rest, 2 * (i + 2))
                eng.wait_ge(sp_logs, i + 2)
                wait(eng, dA_ready, NS * (i + 1))
                tt(dt[:, :, :], sp_relu[:, :, :], sp_log, ALU.add).then_inc(dt_ready, 1)

        def scale_xc(eng, tt, i):
            eng.wait_ge(dt_ready, i + 2)
            wait(eng, w_ready, NS * (i + 1))
            tt(u[:, :, :], dt[:, :, :], xc[:, :, :], ALU.mult).then_inc(u_ready, 1)

        def on_pe(c, n):
            return isinstance(c, int) and c == 0 and n in PE_SUMS

        def add_to_y(eng, tt, i, n):
            g = i * NS + n
            eng.wait_ge(read_out, g + 1)
            if n == 0 or on_pe(i, n - 1):
                eng.wait_ge(y_begun, 2 * (i + 1))
            wait(eng, y_added, g)
            tt(y[:, :, :], y[:, :, :], w[:, n % W_RING, :, :], ALU.add).then_inc(y_added, 1)

        def flat(tile):
            return tile[:, :, :].rearrange("p j d -> p (j d)")

        ITER = list(range(-1, NCH + 2))

        def pipeline(eng, body):
            for i in ITER:
                if i < LOOP0 or i >= LOOP1:
                    body(i)
                elif i == LOOP0:
                    with eng.Fori(LOOP0, LOOP1) as r:
                        body(r)

        N_STAGE = 2 * NE // 2
        PLACES = [k + q / 4 for k in range(SLOTS) for q in range(4)]

        def due(at, place):
            return {place: 0, place - SLOTS: 1, place + SLOTS: -1}.get(at)

        def states(i, table, place):
            found = [(due(at, place), n) for n, at in enumerate(table)]
            return [(i + off, n) for off, n in found if off is not None and has(i, off)]

        def stage_piece(i, place):
            at = {tuple(key): p for p, key in enumerate(STAGE_AT)}
            return at.get((i, place)) if isinstance(i, int) else None

        def unit_at(k):
            return (-2, UNITS - SWITCH + k) if k < SWITCH else (-1, k - SWITCH)

        block = ctx.enter_context(nc.Block())

        @block.sync
        def _(sp):
            sp.dma_start(xf[:, :, :], x_view[0, :, :, :]).then_inc(xf_loaded, DMA)
            sp.dma_start(dtw, dtproj).then_inc(dtw_loaded, DMA)
            sp.dma_start(par[:, :], packed).then_inc(par_loaded, DMA)
            sp.dma_start(win_sb[:, :], win).then_inc(small_loaded, DMA)
            sp.dma_start(xproj_sb[:, :, :], xproj.rearrange("(k p) n -> p k n", p=P)).then_inc(small_loaded, DMA)
            sp.dma_start(wout_sb[:, :, :], wout.rearrange("(k p) n -> p k n", p=P)).then_inc(small_loaded, DMA)
            sp.dma_start(w1_sb[:, :], w1).then_inc(small_loaded, DMA)
            sp.dma_start(w2_sb[:, :, :], w2.rearrange("(k p) n -> p k n", p=P)).then_inc(small_loaded, DMA)
            sp.dma_start(b2_rows[:, :], ffn_b2).then_inc(small_loaded, DMA)

            def one_chunk(view, c):
                return view[bass.ds(c, 1), :, :, :].rearrange("c p j d -> p (c j) d")

            def load_piece(s):
                src = (wg, wu)[s // (NE // 2)]
                e = 2 * (s % (NE // 2))
                wait(sp, stage_lo, s - STAGE_RING + 1)
                sp.dma_start(w_stage[:, s % STAGE_RING, :, :], src[e:e + 2, :, :].rearrange("e p f -> p e f")
                             ).then_inc(stage_loaded[s % STAGE_RING], DMA)

            load_piece(0)
            sp.wait_ge(dtw_steps, 4)
            for row, part in ((BC, dtw_hi), (BC + DTR, dtw_lo), (LO + BC, dtw_hi)):
                sp.dma_start(dtproj_r[row:row + DTR, :].bitcast(F32), part.bitcast(F32)).then_inc(dtw_placed, DMA)
            for s in range(1, STAGE_RING):
                load_piece(s)
            sp.wait_ge(ln_done[0], 1)
            sp.dma_start(xf[:, :, :], x_view[1, :, :, :]).then_inc(xf_loaded, DMA)
            for s in range(STAGE_RING, N_STAGE):
                load_piece(s)
            sp.dma_start(wd_sb[:, :, :, :], wd.rearrange("e (k p) d -> p e k d", p=P)).then_inc(wd_loaded, DMA)

            def body(i):
                if has(i, -1):
                    wait(sp, x1_ready, 3 * (i - 1))
                    sp.dma_start(xb[:, :, :], one_chunk(x_view, i - 1)).then_inc(xb_loaded, DMA)
                if has(i, -2):
                    sp.wait_ge(m_free, m_count(i, "turn4"))
                    sp.dma_start(one_chunk(out_view, i - 2), res[:, :, :]).then_inc(stored, DMA)
                if has(i, 3):
                    wait(sp, ln_done[0], i + 3)
                    sp.dma_start(xf[:, :, :], one_chunk(x_view, i + 3)).then_inc(xf_loaded, DMA)

            for i in ITER:
                if i < LOOP0 or i >= LOOP1 - 1:
                    body(i)
                elif i == LOOP0:
                    with sp.Fori(LOOP0, LOOP1 - 1) as r:
                        body(r)
            sp.wait_ge(stored, DMA * NCH)

        @block.tensor
        def _(pe):
            mm = nc.tensor.matmul

            def m_begin(i, name):
                wait(pe, m_free, m_count(i, name) - 1)

            def turn(dst, src):
                for j in range(NJ):
                    last = nc.tensor.transpose(dst[:, j * P:(j + 1) * P], src[:, j * P:(j + 1) * P], ident[:, :])
                return last

            def spread_b(c, n):
                if n == 0:
                    wait(pe, bc_for_b, c + 1)
                wait(pe, b_copied, c * NS + n)
                mm(ps_b[:, :], pick_r[:, n:n + 1].to_broadcast([XP, P]), bc[:, :],
                   start=True, stop=True).then_inc(b_spread, 1)

            def spread_c(c, n):
                if n == 0:
                    wait(pe, bc_for_c, c + 1)
                wait(pe, read_out, c * NS + n)
                mm(ps_c[:, :], pick_r[:, NS + n:NS + n + 1].to_broadcast([XP, P]), bc_late[:, :],
                   start=True, stop=True).then_inc(c_spread, 1)

            def sum_y(n):
                pe.wait_ge(read_out, n + 1)
                wait(pe, y_added, n)
                for t in range(NT):
                    last = mm(ps_g[:, t, :], ident[:, :], hc0[n % 2][:, t, :],
                              start=(n == min(PE_SUMS)), stop=(n == max(PE_SUMS)))
                last.then_inc(y_added, 1)

            def up(c, k):
                e, f = divmod(k, FT)
                r = k % GU_RING
                g = c * UNITS + k
                if k == 0:
                    wait(pe, m_free, m_count(c + 1, "turn3"))
                if isinstance(c, int) and c == 0 and f == 0 and e % 2 == 0:
                    pe.wait_ge(stage_lo, N_STAGE)
                    pe.wait_ge(y_folded, 1)
                wait(pe, hm_ready, g - GU_RING + 1)
                for bank, hi, lo in ((ps_g, wg_hi, wg_lo), (ps_u, wu_hi, wu_lo)):
                    cols = slice(f * P, (f + 1) * P)
                    mm(bank[:, r, :], hi[:, e, cols], x_hi[:, :], start=True, stop=False)
                    mm(bank[:, r, :], hi[:, e, cols], x_lo[:, :], start=False, stop=False)
                    last = mm(bank[:, r, :], lo[:, e, cols], x_hi[:, :], start=False, stop=True)
                last.then_inc(gu_full, 1)

            def down(c, k):
                e, f = divmod(k, FT)
                if k == 0:
                    wait(pe, yT_ready, c)
                    if isinstance(c, int) and c == 0:
                        pe.wait_ge(wd_loaded, DMA)
                    mm(ps_y[:, :], ident_r[:, :], x_hi[:, :], start=True, stop=False)
                    mm(ps_y[:, :], ident_r[:, :], x_lo[:, :], start=False, stop=False)
                wait(pe, hm_ready, c * UNITS + k + 1)
                mm(ps_y[:, :], wd_sb[:, e, f, :], hm[:, k % HM_RING, :], start=False,
                   stop=(k == UNITS - 1)).then_inc(down_done, 1)

            def misc(i, name):
                m_begin(i, name)
                if name in ("z0", "z1"):
                    t = int(name[1])
                    mm(ps_m[:, :], win_sb[:, DI + t * P:DI + (t + 1) * P], xnT[:, :],
                       start=True, stop=True).then_inc(m_full, 1)
                elif name in ("xi0", "xi1"):
                    if name == "xi0":
                        wait(pe, m_free, m_count(i, "turn1"))
                    t = int(name[2])
                    mm(ps_m[:, :], win_sb[:, t * P:(t + 1) * P], xnT[:, :],
                       start=True, stop=True).then_inc(m_full, 1)
                elif name == "turn1":
                    wait(pe, ln_done[0], i + 2)
                    turn(ps_m, xn1[:, :, :].rearrange("p j d -> p (j d)")).then_inc(m_full, 1)
                elif name == "x_proj":
                    wait(pe, xc_ready, 2 * (i + 2))
                    for t in range(NT):
                        last = mm(ps_m[0:XP, :], xproj_sb[:, t, :], xc[:, t, :], start=(t == 0), stop=(t == NT - 1))
                    last.then_inc(m_full, 1)
                elif name in ("dt0", "dt1"):
                    t = int(name[2])
                    wait(pe, bc_lo, i + 2)
                    if first(i):
                        pe.wait_ge(dtw_placed, 3 * DMA)
                    mm(ps_m[:, :], dtproj_r[:, t * P:(t + 1) * P], bc_new[:, :],
                       start=True, stop=True).then_inc(m_full, 1)
                elif name == "out_proj":
                    wait(pe, y2_ready, i)
                    for j in range(NJ):
                        for t in range(NT):
                            last = mm(ps_m[:, j * P:(j + 1) * P], y2[:, t, j * P:(j + 1) * P], wout_sb[:, t, :],
                                      start=(t == 0), stop=(t == NT - 1))
                    last.then_inc(m_full, 1)
                elif name in ("turn2", "turn3"):
                    k = int(name[4]) - 1
                    wait(pe, ln_done[k], i)
                    turn(ps_m, xn2[:, :, :].rearrange("p j d -> p (j d)")).then_inc(m_full, 1)
                elif name.startswith("ffn1_"):
                    t = int(name[5])
                    wait(pe, m_free, m_count(i, "turn2"))
                    mm(ps_m[:, :], w1_sb[:, t * P:(t + 1) * P], hT[:, :], start=True, stop=True).then_inc(m_full, 1)
                elif name == "ffn2":
                    wait(pe, m_free, m_count(i, "ffn1_3"))
                    for j in range(NJ):
                        for t in range(FFT):
                            last = mm(ps_m[:, j * P:(j + 1) * P], fh[:, t, j * P:(j + 1) * P], w2_sb[:, t, :],
                                      start=(t == 0), stop=(t == FFT - 1))
                    last.then_inc(m_full, 1)
                elif name == "turn4":
                    wait(pe, yT_ready, i - 1)
                    turn(ps_m, yT).then_inc(m_full, 1)

            def body(i):
                for place in PLACES:
                    for c, n in states(i, SPREAD_C_AT, place):
                        spread_c(c, n)
                        if on_pe(c, n - 1):
                            sum_y(n - 1)
                    if place == PLACES[-1] and on_pe(i, NS - 1):
                        sum_y(NS - 1)
                    for c, n in states(i, SPREAD_B_AT, place):
                        spread_b(c, n)
                    for j, at in enumerate(DOWN_AT):
                        off, unit = unit_at(j)
                        later = due(at, place)
                        if later is not None and has(i, off + later):
                            down(i + off + later, unit)
                    for name, off in M_USES:
                        if PE_AT[name] == place and has(i, off):
                            misc(i, name)
                    if place % 1 == .25:
                        off, unit = unit_at(int(place))
                        if has(i, off):
                            up(i + off, unit)

            pe.wait_ge(consts_made, 3)
            pe.wait_ge(small_loaded, 6 * DMA)
            pipeline(pe, body)

        @block.scalar
        def _(act):
            fn = nc.scalar.activation

            def m_wait(i, name):
                act.wait_ge(m_full, m_count(i, name))

            def exps(c, n):
                g = c * NS + n
                wait(act, scanned, g - DA_RING + 1)
                for t in range(NT):
                    last = fn(dA[:, n % DA_RING, t, :, 1:L],
                              dt[:, t, :].rearrange("p (b l) -> p b l", b=NB)[:, :, 1:L],
                              ACT.Exp, scale=a_neg[:, t, n:n + 1])
                last.then_inc(dA_ready, 1)

            def burst(i, q):
                c, n0 = (i, (q + 1) * BURST) if q < 3 else (i + 1, 0)
                if q == 3:
                    wait(act, dt_ready, i + 2)
                for n in range(n0, n0 + BURST):
                    exps(c, n)

            def softplus_exp(i):
                act.wait_ge(sp_abs, 2 * (i + 2))
                fn(sp_exp, sp_exp, ACT.Exp, scale=-1.0).then_inc(sp_exps, 1)

            def softplus_log(i):
                act.wait_ge(sp_exps, i + 2)
                fn(sp_log, sp_exp, ACT.Ln, bias=1.0).then_inc(sp_logs, 1)

            def silu(c, k):
                g = c * UNITS + k
                act.wait_ge(gu_full, g + 1)
                wait(act, hm_ready, g - SG_RING + 1)
                fn(sg[:, k % SG_RING, :], ps_g[:, k % GU_RING, :], ACT.Silu).then_inc(silu_ready, 1)

            def copy_b(c, n):
                g = c * NS + n
                act.wait_ge(b_spread, g + 1)
                wait(act, w_ready, g - 1)
                fn(b_rep[:, n % 2, :], ps_b[:, :], ACT.Copy).then_inc(b_copied, 1)

            def ln_norm(k, c, dst, src):
                act.wait_ge(ln_rstd[k], c + 1)
                act.wait_ge(ln_shift[k], c + 1)
                for j in range(NJ):
                    last = fn(dst[:, j, :], src[:, j * P:(j + 1) * P], ACT.Identity,
                              scale=rstd[:, k, j:j + 1], bias=shift[:, k, j:j + 1])
                return last

            def norm(i, k):
                if k == 1 and has(i, 2):
                    if has(i, 1):
                        act.wait_ge(m_full, m_count(i, "turn1"))
                    if has(i, -1):
                        act.wait_ge(m_full, m_count(i, "ffn1_3"))
                    ln_norm(0, i + 2, xn1, flat(xf)).then_inc(ln_done[0], 1)
                elif k == 2 and has(i, -1):
                    ln_norm(1, i - 1, xn2, flat(x1)).then_inc(ln_done[1], 1)
                elif k == 3 and has(i, -1):
                    ln_norm(2, i - 1, xn2, flat(x1)).then_inc(ln_done[2], 1)
                elif k == 4 and has(i, -2):
                    wait(act, stored, DMA * (i - 2))
                    ln_norm(3, i - 2, res, ps_m[:, :]).then_inc(m_free, 1)

            def begin_y(i):
                wait(act, y2_ready, i)
                for t in range(NT):
                    fn(y[:, t, :], xc[:, t, :], ACT.Copy, scale=col("D", t)).then_inc(y_begun, 1)

            def misc(i, name):
                m_wait(i, name)
                if name in ("z0", "z1"):
                    t = int(name[1])
                    wait(act, y2_ready, i)
                    fn(sz[:, t, :], ps_m[:, :], ACT.Silu).then_inc(m_free, 1)
                elif name == "turn1":
                    fn(xnT[:, :], ps_m[:, :], ACT.Identity, scale=col("g1"), bias=col("b1")).then_inc(m_free, 1)
                elif name in ("xi0", "xi1"):
                    t = int(name[2])
                    wait(act, sp_rest, 2 * (i + 1))
                    wait(act, u_ready, i + 1)
                    v = ps_m[:, :].rearrange("p (b l) -> p b l", b=NB)
                    fn(xi[:, t, :, TAPS - 1:], v, ACT.Copy)
                    fn(xc[:, t, :].rearrange("p (b l) -> p b l", b=NB), v, ACT.Copy,
                       scale=col("conv_w", TAPS * t + TAPS - 1)).then_inc(m_free, 1)
                elif name == "x_proj":
                    wait(act, bc_lo, i + 1)
                    fn(bcdt[:, :], ps_m[0:XP, :], ACT.Copy).then_inc(m_free, 1)
                elif name in ("dt0", "dt1"):
                    t = int(name[2])
                    if t == 0:
                        wait(act, dt_ready, i + 1)
                        if has(i, -1):
                            wait(act, m_full, m_count(i, "ffn2"))
                    fn(sp_exp[:, t, :], ps_m[:, :], ACT.Abs, bias=col("dt_b", t)).then_inc(sp_abs, 1)
                    fn(sp_relu[:, t, :], ps_m[:, :], ACT.Relu, bias=col("dt_b", t)).then_inc(m_free, 1)
                elif name == "turn2":
                    fn(hT[:, :], ps_m[:, :], ACT.Identity, scale=col("g2"), bias=col("b2")).then_inc(m_free, 1)
                elif name.startswith("ffn1_"):
                    t = int(name[5])
                    if t == 0 and has(i, 0):
                        wait(act, dt_ready, i + 1)
                    fn(fh[:, t, :], ps_m[:, :], ACT.Relu, bias=col("ffn_b1", t)).then_inc(m_free, 1)
                elif name == "turn3":
                    wait(act, gu_full, UNITS * (i - 1))
                    fn(x_hi[:, :], ps_m[:, :], ACT.Copy).then_inc(x_hi_ready, 1)

            def split_hi(s):
                dst = (wg_hi, wu_hi)[s // (NE // 2)]
                e = 2 * (s % (NE // 2))
                act.wait_ge(stage_loaded[s % STAGE_RING], DMA * (s // STAGE_RING + 1))
                fn(dst[:, e:e + 2, :], w_stage[:, s % STAGE_RING, :, :], ACT.Copy).then_inc(stage_hi, 1)

            def conv_silu(i, t):
                act.wait_ge(conv_taps, (TAPS - 1) * (2 * (i + 1) + t + 1))
                fn(xc[:, t, :], xc[:, t, :], ACT.Silu, bias=col("conv_b", t)).then_inc(xc_ready, 1)

            def body(i):
                for place in PLACES:
                    for c, n in states(i, COPY_B_AT, place):
                        if not (first(i) and n == 0):
                            copy_b(c, n)
                    if place == ACT_AT["begin_y"] and has(i, 0) and not first(i - 1):
                        begin_y(i)
                    if place in BURST_AT:
                        q = BURST_AT.index(place)
                        if q == 3 and first(i):
                            begin_y(0)
                            copy_b(0, 0)
                        if has(i, 0 if q < 3 else 1):
                            burst(i, q)
                    if place == ACT_AT["softplus_exp"] and has(i, 1):
                        softplus_exp(i)
                    for k in range(1, 5):
                        if place == ACT_AT[f"norm{k}"]:
                            norm(i, k)
                    if place == ACT_AT["yT"] and has(i, -2):
                        act.wait_ge(down_done, UNITS * (i - 1))
                        fn(yT, ps_y[:, :], ACT.Copy).then_inc(yT_ready, 1)
                    for name, off in M_USES:
                        if ACT_AT.get(name) == place and has(i, off):
                            misc(i, name)
                    for t in range(NT):
                        if place == ACT_AT[f"conv_silu{t}"] and has(i, 1):
                            conv_silu(i, t)
                    if place == ACT_AT["softplus_log"] and has(i, 1):
                        softplus_log(i)
                    if stage_piece(i, place) is not None:
                        split_hi(stage_piece(i, place))
                    if place % 1 == .25:
                        off, unit = unit_at(int(place))
                        if has(i, off):
                            silu(i + off, unit)

            act.wait_ge(par_loaded, DMA)
            lo, hi = PACK["A_log"]
            fn(a_neg[:, :, :].rearrange("p t n -> p (t n)"), par[:, lo:hi], ACT.Exp).then_inc(a_exp, 1)
            act.wait_ge(a_made, 1)
            ln_norm(0, 0, xn1, flat(xf)).then_inc(ln_done[0], 1)
            act.wait_ge(ring_zeroed, 1)
            act.wait_ge(pads_zeroed, 1)
            pipeline(act, body)

        @block.vector
        def _(dve):
            tt, ts, stt = nc.vector.tensor_tensor, nc.vector.tensor_scalar, nc.vector.scalar_tensor_tensor

            def ln_stats(k, c, src):
                for j in range(NJ):
                    last = nc.vector.bn_stats(stats[:, k, j, :], src[:, j * P:(j + 1) * P])
                last.then_inc(ln_steps[k], 1)
                dve.wait_ge(ln_steps[k], 2 * c + 1)
                dve.sem_inc(aggr_held, 1)
                for j in range(NJ):
                    last = nc.vector.bn_aggr(mv[:, k, j, :], stats[:, k, j, :])
                last.then_inc(ln_steps[k], 1)
                dve.wait_ge(ln_steps[k], 2 * c + 2)
                ts(ve[:, k, :], mv[:, k, :, 1], EPS, None, ALU.add).then_inc(ln_var[k], 1)

            def scan(i, n):
                g = i * NS + n
                dve.wait_ge(dA_ready, g + 1)
                dve.wait_ge(w_ready, g + 1)
                wait(dve, read_out, g)
                nc.vector.tensor_tensor_scan(
                    flat(h), dA[:, n % DA_RING, :, :, :].rearrange("p t b l -> p (t b l)"),
                    w[:, n % W_RING, :, :].rearrange("p t l -> p (t l)"), 0.0, ALU.mult, ALU.add).then_inc(scanned, 1)

            def read(i, n):
                g = i * NS + n
                dve.wait_ge(scanned, g + 1)
                dve.wait_ge(c_spread, g + 1)
                dst = w[:, n % W_RING, :, :]
                if on_pe(i, n):
                    dst = hc0[n % 2][:, :, :]
                    wait(dve, y_added, g - 1)
                tt(dst, h[:, :, :], ps_c[:, :].unsqueeze(1).to_broadcast([P, NT, TOK]),
                   ALU.mult).then_inc(read_out, 1)

            def gate(i):
                if isinstance(i, int) and i == 1:
                    dve.wait_ge(y_added, NS)
                    dve.wait_ge(y_begun, 2)
                    tt(y[:, :, :], y[:, :, :], ps_g[:, :, :], ALU.add).then_inc(y_folded, 1)
                    dve.wait_ge(y_folded, 1)
                dve.wait_ge(y_added, NS * i)
                dve.wait_ge(m_free, m_count(i - 1, "z1"))
                if has(i, 0):
                    dve.wait_ge(dt_ready, i + 1)
                tt(y2, y[:, :, :], sz[:, :, :], ALU.mult).then_inc(y2_ready, 1)

            def residual1(i):
                dve.wait_ge(xb_loaded, DMA * i)
                dve.wait_ge(m_full, m_count(i, "out_proj"))
                tt(flat(x1), flat(xb), ps_m[:, :], ALU.add).then_inc(m_free, 1)
                dve.wait_ge(m_free, m_count(i, "out_proj"))
                ln_stats(1, i - 1, flat(x1))

            def residual3(i):
                dve.wait_ge(x1_ready, 3 * i)
                dve.wait_ge(m_full, m_count(i, "ffn2"))
                tt(flat(x1), flat(x1), ps_m[:, :], ALU.add).then_inc(m_free, 1)
                dve.wait_ge(m_free, m_count(i, "ffn2"))
                ln_stats(2, i - 1, flat(x1))

            def conv(i, t):
                dve.wait_ge(m_free, m_count(i, f"xi{t}"))
                acc = xc[:, t, :].rearrange("p (b l) -> p b l", b=NB)
                for k in range(TAPS - 1):
                    if k:
                        dve.wait_ge(conv_taps, (TAPS - 1) * (2 * (i + 1) + t) + k)
                    stt(acc, xi[:, t, :, k:k + L], col("conv_w", TAPS * t + k), acc,
                        ALU.mult, ALU.add).then_inc(conv_taps, 1)

            def times(c, k):
                g = c * UNITS + k
                dve.wait_ge(silu_ready, g + 1)
                wait(dve, down_done, g - HM_RING + 1)
                tt(hm[:, k % HM_RING, :], sg[:, k % SG_RING, :], ps_u[:, k % GU_RING, :], ALU.mult).then_inc(hm_ready, 1)

            def split_bc(i):
                dve.wait_ge(m_free, m_count(i, "x_proj"))
                if has(i, 0):
                    dve.wait_ge(m_full, m_count(i - 1, "dt1"))
                    dve.wait_ge(bc_for_c, i + 1)
                nc.vector.tensor_copy(bc_new[:, :], bcdt[:, :]).then_inc(bc_hi, 1)
                dve.wait_ge(bc_hi, i + 2)
                tt(bc_new[LO:XP, :], bcdt[LO:XP, :], bc_new[LO:XP, :].bitcast(F32), ALU.subtract).then_inc(bc_lo, 1)

            def step(i, name):
                if name == "gate" and has(i, -1):
                    gate(i)
                elif name == "split_bc" and has(i, 1):
                    split_bc(i)
                elif name == "residual1" and has(i, -1):
                    residual1(i)
                elif name == "x_lo" and has(i, -1):
                    dve.wait_ge(x_hi_ready, i)
                    tt(x_lo[:, :], ps_m[:, :], x_hi[:, :].bitcast(F32), ALU.subtract).then_inc(m_free, 1)
                elif name in ("conv0", "conv1") and has(i, 1):
                    conv(i, int(name[4]))
                elif name == "residual3" and has(i, -1):
                    residual3(i)
                elif name == "sp_round" and has(i, 1):
                    dve.wait_ge(sp_exps, i + 2)
                    ts(xi[:, :, :, TAPS - 1:], sp_exp.rearrange("p t (b l) -> p t b l", b=NB), 1.0, -1.0,
                       ALU.add, ALU.add).then_inc(sp_round, 1)
                    if first(i):
                        for part in range(3):
                            softplus_sum(dve, tt, i, part)
                        scale_xc(dve, tt, i)
                elif name == "stats4" and has(i, -2):
                    dve.wait_ge(m_full, m_count(i, "turn4"))
                    ln_stats(3, i - 2, ps_m[:, :])
                elif name == "stats1" and has(i, 2):
                    dve.wait_ge(xf_loaded, DMA * (i + 3))
                    ln_stats(0, i + 2, flat(xf))

            def body(i):
                for place in PLACES:
                    for c, n in states(i, SCAN_AT, place):
                        scan(c, n)
                    for c, n in states(i, READ_AT, place):
                        read(c, n)
                    for c, n in states(i, ADD_AT, place):
                        if n not in POOL_ADDS and not on_pe(c, n):
                            add_to_y(dve, tt, c, n)
                    for name, at in DVE_AT.items():
                        if at == place:
                            step(i, name)
                    if place % 1 == .25:
                        off, unit = unit_at(int(place))
                        if has(i, off):
                            times(i + off, unit)

            dve.wait_ge(xf_loaded, DMA)
            ln_stats(0, 0, flat(xf))
            dve.wait_ge(dtw_loaded, DMA)
            nc.vector.tensor_copy(dtw_hi, dtw).then_inc(dtw_steps, 1)
            dve.wait_ge(dtw_steps, 1)
            tt(dtw_lo, dtw, dtw_hi.bitcast(F32), ALU.subtract).then_inc(dtw_steps, 1)
            zeros = flat(res)[0:XP, 0:DI]
            nc.vector.memset(zeros, 0.0).then_inc(dtw_steps, 1)
            dve.wait_ge(dtw_steps, 3)
            nc.vector.tensor_copy(dtproj_r[:, :], zeros).then_inc(dtw_steps, 1)
            nc.vector.memset(dA[:, :, :, :, 0:1], 0.0).then_inc(ring_zeroed, 1)
            nc.vector.memset(xi[:, :, :, 0:TAPS - 1], 0.0).then_inc(pads_zeroed, 1)
            dve.wait_ge(a_exp, 1)
            ts(a_neg[:, :, :], a_neg[:, :, :], -1.0, None, ALU.mult).then_inc(a_made, 1)
            pipeline(dve, body)

        @block.gpsimd
        def _(pool):
            tt = nc.gpsimd.tensor_tensor

            def rsqrt(k, c):
                pool.wait_ge(ln_var[k], c + 1)
                tt(minus_mean[:, k, :], mv[:, k, :, 0], minus_one[:, :], ALU.mult).then_inc(ln_minus[k], 1)
                tt(rstd[:, k, :], ve[:, k, :], minus_half[:, :], ALU.pow).then_inc(ln_rstd[k], 1)
                pool.wait_ge(ln_minus[k], c + 1)
                pool.wait_ge(ln_rstd[k], c + 1)
                tt(shift[:, k, :], minus_mean[:, k, :], rstd[:, k, :], ALU.mult).then_inc(ln_shift[k], 1)

            def dbx(c, n):
                g = c * NS + n
                pool.wait_ge(b_copied, g + 1)
                if on_pe(c, n - W_RING):
                    wait(pool, scanned, g - W_RING + 1)
                else:
                    wait(pool, y_added, g - W_RING + 1)
                if n == 0:
                    pool.wait_ge(u_ready, c + 1)
                tt(w[:, n % W_RING, :, :], u[:, :, :], b_rep[:, n % 2, :].unsqueeze(1).to_broadcast([P, NT, TOK]),
                   ALU.mult).then_inc(w_ready, 1)

            def residual2(i):
                pool.wait_ge(ln_done[1], i)
                tt(x1[:, :, :], x1[:, :, :], xb[:, :, :], ALU.add).then_inc(x1_ready, 1)
                pool.wait_ge(x1_ready, 3 * (i - 1) + 1)
                tt(x1[:, :, :], x1[:, :, :], b2_rows[:, :].unsqueeze(1).to_broadcast([P, NJ, DM]),
                   ALU.add).then_inc(x1_ready, 2)

            def copy_bc(i, name):
                pool.wait_ge(bc_lo, i + 2)
                dst, spread, done = {"for_b": (bc, b_spread, bc_for_b), "for_c": (bc_late, c_spread, bc_for_c)}[name]
                wait(pool, spread, NS * (i + 1))
                tt(dst[:, :], bc_new[:, :].bitcast(F32), one[0:XP, :].to_broadcast([XP, TOK]), ALU.mult).then_inc(done, 1)

            def split_lo(s):
                hi, lo = ((wg_hi, wg_lo), (wu_hi, wu_lo))[s // (NE // 2)]
                e = 2 * (s % (NE // 2))
                pool.wait_ge(stage_hi, s + 1)
                tt(lo[:, e:e + 2, :], w_stage[:, s % STAGE_RING, :, :], hi[:, e:e + 2, :].bitcast(F32),
                   ALU.subtract).then_inc(stage_lo, 1)

            def step(i, name):
                if name.startswith("rsqrt"):
                    ln = int(name[5]) - 1
                    off = (2, -1, -1, -2)[ln]
                    if has(i, off):
                        rsqrt(ln, i + off)
                elif name.startswith("sp_sum") and has(i, 1) and not first(i):
                    softplus_sum(pool, tt, i, int(name[6]))
                elif name == "residual2" and has(i, -1):
                    residual2(i)
                elif name == "scale_xc" and has(i, 1) and not first(i):
                    scale_xc(pool, tt, i)
                elif name in ("for_b", "for_c") and has(i, 1):
                    copy_bc(i, name)

            def body(i):
                for place in PLACES:
                    for c, n in states(i, ADD_AT, place):
                        if n in POOL_ADDS and not on_pe(c, n):
                            add_to_y(pool, tt, c, n)
                    for c, n in states(i, DBX_AT, place):
                        dbx(c, n)
                    for name, at in POOL_AT.items():
                        if at == place:
                            step(i, name)
                    if stage_piece(i, place) is not None:
                        split_lo(stage_piece(i, place))

            nc.gpsimd.memset(minus_half[:, :], -0.5).then_inc(halves_made, 1)
            nc.gpsimd.memset(minus_one[:, :], -1.0).then_inc(halves_made, 1)
            nc.gpsimd.memset(one[:, :], 1.0).then_inc(halves_made, 1)
            nc.gpsimd.memset(ident[:, :], 0.0).then_inc(ident_steps, 1)
            nc.gpsimd.memset(pick[:, :], 0.0).then_inc(ident_steps, 1)
            pool.wait_ge(ident_steps, 2)
            nc.gpsimd.affine_select(out=ident[:, :], in_=ident[:, :], compare_op=ALU.not_equal, fill=1.0,
                                    base=0, pattern=[[-1, P]], channel_multiplier=1).then_inc(consts_made, 1)
            for part in range(2):
                nc.gpsimd.affine_select(out=pick[:, :], in_=pick[:, :], compare_op=ALU.not_equal, fill=1.0,
                                        base=-part * LO, pattern=[[-1, BC]], channel_multiplier=1).then_inc(ident_steps, 1)
                pool.wait_ge(ident_steps, 3 + part)
            pool.wait_ge(consts_made, 1)
            pool.wait_ge(halves_made, 3)
            rsqrt(0, 0)
            nc.gpsimd.tensor_copy(ident_r[:, :], ident[:, :]).then_inc(consts_made, 1)
            nc.gpsimd.tensor_copy(pick_r[:, :], pick[:, :]).then_inc(consts_made, 1)
            pipeline(pool, body)


def kernel(L0_attn_x, L0_attn_in_proj_w, L0_attn_conv_w, L0_attn_conv_b, L0_attn_x_proj_w, L0_attn_dt_proj_w,
           L0_attn_dt_proj_b, L0_attn_A_log, L0_attn_D, L0_attn_out_proj_w, L0_attn_ln1_g, L0_attn_ln1_b,
           L0_attn_ln2_g, L0_attn_ln2_b, L0_attn_ffn_w1, L0_attn_ffn_b1, L0_attn_ffn_w2, L0_attn_ffn_b2,
           L0_ffn_Wg, L0_ffn_Wu, L0_ffn_Wd):
    import numpy as np
    import concourse.bacc as bacc
    from concourse.bass_utils import run_bass_kernel_spmd

    def channels(a, tail=1):
        a = np.asarray(a).reshape(-1, P, tail)
        return a.transpose(1, 0, 2).reshape(P, -1)

    parts = {
        "g1": channels(L0_attn_ln1_g), "b1": channels(L0_attn_ln1_b),
        "g2": channels(L0_attn_ln2_g), "b2": channels(L0_attn_ln2_b),
        "conv_w": channels(L0_attn_conv_w, 4), "conv_b": channels(L0_attn_conv_b),
        "dt_b": channels(L0_attn_dt_proj_b), "D": channels(L0_attn_D),
        "ffn_b1": channels(L0_attn_ffn_b1), "A_log": channels(L0_attn_A_log, 16),
    }
    xp = np.asarray(L0_attn_x_proj_w)
    rank = np.asarray(L0_attn_dt_proj_w).shape[1]
    arrays = {
        "x": np.asarray(L0_attn_x),
        "packed": np.concatenate([parts[k] for k in PACK], axis=1),
        "win": np.asarray(L0_attn_in_proj_w).T,
        "xproj": np.concatenate([xp[rank:], xp[:rank], xp[:rank], np.zeros_like(xp, shape=(64 - len(xp) - rank, xp.shape[1])),
                                 xp[rank:], xp[:rank]], axis=0).T,
        "dtproj": np.asarray(L0_attn_dt_proj_w).T,
        "wout": np.asarray(L0_attn_out_proj_w).T,
        "w1": np.asarray(L0_attn_ffn_w1).T,
        "w2": np.asarray(L0_attn_ffn_w2).T,
        "ffn_b2": np.broadcast_to(np.asarray(L0_attn_ffn_b2), (P, P)),
        "wg": np.asarray(L0_ffn_Wg), "wu": np.asarray(L0_ffn_Wu), "wd": np.asarray(L0_ffn_Wd),
    }
    arrays = {k: np.ascontiguousarray(v) for k, v in arrays.items()}
    nc = bacc.Bacc("TRN2", target_bir_lowering=False, num_devices=1, dynamic_dma_scratch_size=1024)
    args = {k: nc.dram_tensor(k, v.shape, mybir.dt.from_np(v.dtype), kind="ExternalInput").ap()
            for k, v in arrays.items()}
    out = nc.dram_tensor("out", arrays["x"].shape, F32, kind="ExternalOutput").ap()
    build(nc, **args, out=out)
    r = run_bass_kernel_spmd(nc, [arrays], core_ids=[0])
    return r.results[0]["out"]
```
